# Optimizing a Trainium2 kernel written in Bass

```python
import numpy as np
import jax
import jax.numpy as jnp

def _softmax(x, axis=-1):
    return jax.nn.softmax(x, axis=axis)

def _gelu(x):
    return jax.nn.gelu(x, approximate=True)

def _silu(x):
    return jax.nn.silu(x)

def _sigmoid(x):
    return jax.nn.sigmoid(x)

def _layernorm(x, axis=-1, eps=1e-05):
    m = jnp.mean(x, axis=axis, keepdims=True)
    v = jnp.var(x, axis=axis, keepdims=True)
    return (x - m) / jnp.sqrt(v + eps)

def _scatter_add(tgt, idx, src, axis=0):
    return tgt.at[idx].add(src)

def _segment_sum(src, seg, n):
    return jax.ops.segment_sum(src, seg, n)
kernel_name = 'mk_gnn_ffn_d4_gnn_r16_22e692'

def setup_inputs(seed: int=0):
    np.random.seed(seed)
    _w = jnp.asarray

    def _rec_inputs():
        import jax
        import jax.numpy as jnp
        _gk = jax.random.key(seed)
        x = -0.0003713 + 1 * jax.random.normal(jax.random.fold_in(_gk, 1), (3125, 256), jnp.float32)
        src = jax.random.randint(jax.random.fold_in(_gk, 2), (50000,), 0, 3125, jnp.int32)
        dst = jnp.minimum((3125 * jax.random.uniform(jax.random.fold_in(_gk, 3), (50000,)) ** 2.0).astype(jnp.int32), 49999)
        _o = jnp.argsort(dst, stable=True)
        src = src[_o]
        dst = dst[_o]
        edge_attr_256 = 2.93046e-05 + 1.00006 * jax.random.normal(jax.random.fold_in(_gk, 11), (50000, 256), jnp.float32)
        return (x, src, dst, edge_attr_256)
    x, src, dst, edge_attr_256 = _rec_inputs()

    def _L0_gnn_setup():
        import jax, jax.numpy as jnp
        import numpy as np
        N_NODES = 3125
        N_EDGES = 100000
        H_SIZE = 256
        HEADS = 8
        HEAD_DIM = H_SIZE // HEADS
        NEG_SLOPE = 0.2
        key = jax.random.key(seed)
        k_x, k_e, k_w, k_as, k_ad, k_b = jax.random.split(key, 6)
        x = jax.random.normal(k_x, (N_NODES, H_SIZE), dtype=jnp.float32)
        edge_index = jax.random.randint(k_e, (2, N_EDGES), 0, N_NODES, dtype=jnp.int64)
        scale = 1.0 / np.sqrt(H_SIZE)
        W = jax.random.normal(k_w, (H_SIZE, HEADS, HEAD_DIM), dtype=jnp.float32) * scale
        att_src = jax.random.normal(k_as, (HEADS, HEAD_DIM), dtype=jnp.float32) * scale
        att_dst = jax.random.normal(k_ad, (HEADS, HEAD_DIM), dtype=jnp.float32) * scale
        bias = jnp.zeros((H_SIZE,), dtype=jnp.float32)
        return {'x': x, 'edge_index': edge_index, 'W': W, 'att_src': att_src, 'att_dst': att_dst, 'bias': bias}
    _L0_gnn_all = _L0_gnn_setup()
    _L0_gnn_in = {k: v for k, v in _L0_gnn_all.items() if k in ('W', 'att_src', 'att_dst', 'bias')}
    del _L0_gnn_all

    def _L0_ffn_setup():
        import jax, jax.numpy as jnp
        import numpy as np
        B, S, H, F, E, K = (8, 256, 256, 512, 16, 2)
        EPS = 1e-05
        key = jax.random.key(seed)
        ks = jax.random.split(key, 9)
        sc = 0.02
        return {'x': jax.random.normal(ks[0], (B, S, H), dtype=jnp.float32), 'gate_w': jax.random.normal(ks[1], (H, E), dtype=jnp.float32) * sc, 'gate_b': jnp.zeros((E,), dtype=jnp.float32), 'w1': jax.random.normal(ks[2], (E, H, F), dtype=jnp.float32) * sc, 'b1': jnp.zeros((E, F), dtype=jnp.float32), 'w2': jax.random.normal(ks[3], (E, F, H), dtype=jnp.float32) * sc, 'b2': jnp.zeros((E, H), dtype=jnp.float32), 'gamma': jnp.ones((H,), dtype=jnp.float32), 'beta': jnp.zeros((H,), dtype=jnp.float32)}
    _L0_ffn_all = _L0_ffn_setup()
    _L0_ffn_in = {k: v for k, v in _L0_ffn_all.items() if k in ('gate_w', 'gate_b', 'w1', 'b1', 'w2', 'b2', 'gamma', 'beta')}
    del _L0_ffn_all

    def _L1_gnn_setup():
        import jax, jax.numpy as jnp
        import numpy as np
        NEG_SLOPE = 0.2
        EPS = 1e-08
        N, E, IN_F, OUT_F, H = (3125, 50000, 256, 32, 8)
        key = jax.random.key(seed)
        k1, k2, k3, k4, k5 = jax.random.split(key, 5)
        x = jax.random.normal(k1, (N, IN_F), dtype=jnp.float32)
        edge_index = jax.random.randint(k2, (2, E), 0, N, dtype=jnp.int32)
        bw = float(np.sqrt(6.0 / (IN_F + OUT_F)))
        W = jax.random.uniform(k3, (H, IN_F, OUT_F), minval=-bw, maxval=bw, dtype=jnp.float32)
        ba = float(np.sqrt(6.0 / (OUT_F + 1)))
        a_src = jax.random.uniform(k4, (H, OUT_F), minval=-ba, maxval=ba, dtype=jnp.float32)
        a_dst = jax.random.uniform(k5, (H, OUT_F), minval=-ba, maxval=ba, dtype=jnp.float32)
        return {'x': x, 'edge_index': edge_index, 'W': W, 'a_src': a_src, 'a_dst': a_dst}
    _L1_gnn_all = _L1_gnn_setup()
    _L1_gnn_in = {k: v for k, v in _L1_gnn_all.items() if k in ('W', 'a_src', 'a_dst')}
    del _L1_gnn_all

    def _L1_ffn_setup():
        import math
        import jax, jax.numpy as jnp
        import numpy as np
        CAPACITY_FACTOR = 1.25
        TOP_K = 2
        LN_EPS = 1e-05

        def _layer_norm(x, gamma, beta):
            mu = jnp.mean(x, axis=-1, keepdims=True)
            var = jnp.var(x, axis=-1, keepdims=True)
            return (x - mu) * jax.lax.rsqrt(var + LN_EPS) * gamma + beta
        key = jax.random.key(seed)
        ks = jax.random.split(key, 4)
        B, S, D, F, E = (8, 256, 256, 512, 8)
        x = jax.random.normal(ks[0], (B, S, D), dtype=jnp.float32)
        Wr = jax.random.normal(ks[1], (D, E), dtype=jnp.float32) / np.sqrt(D)
        br = jnp.zeros((E,), jnp.float32)
        W1 = jax.random.normal(ks[2], (E, D, F), dtype=jnp.float32) / np.sqrt(D)
        b1 = jnp.zeros((E, F), jnp.float32)
        W2 = jax.random.normal(ks[3], (E, F, D), dtype=jnp.float32) / np.sqrt(F)
        b2 = jnp.zeros((E, D), jnp.float32)
        gamma = jnp.ones((D,), jnp.float32)
        beta = jnp.zeros((D,), jnp.float32)
        return {'x': x, 'Wr': Wr, 'br': br, 'W1': W1, 'b1': b1, 'W2': W2, 'b2': b2, 'gamma': gamma, 'beta': beta}
    _L1_ffn_all = _L1_ffn_setup()
    _L1_ffn_in = {k: v for k, v in _L1_ffn_all.items() if k in ('Wr', 'br', 'W1', 'b1', 'W2', 'b2', 'gamma', 'beta')}
    del _L1_ffn_all

    def _L2_gnn_setup():
        import jax, jax.numpy as jnp
        import numpy as np
        N_NODES = 3125
        EMB = 256
        HEADS = 8
        NEG_SLOPE = 0.2

        def gat_conv(x, src, dst, W, a_src, a_dst, b, num_nodes):
            h = jnp.einsum('nd,dhf->nhf', x, W)
            al_s = jnp.sum(h * a_src, axis=-1)
            al_d = jnp.sum(h * a_dst, axis=-1)
            logits = jax.nn.leaky_relu(al_s[src] + al_d[dst], NEG_SLOPE)
            m = jax.ops.segment_max(logits, dst, num_segments=num_nodes)
            e = jnp.exp(logits - m[dst])
            z = jax.ops.segment_sum(e, dst, num_segments=num_nodes)
            alpha = e / (z[dst] + 1e-16)
            msg = h[src] * alpha[..., None]
            out = jax.ops.segment_sum(msg, dst, num_segments=num_nodes)
            return out.reshape(num_nodes, -1) + b
        key = jax.random.key(seed)
        ks = jax.random.split(key, 10)
        F1 = EMB // HEADS
        x = jax.random.normal(ks[0], (N_NODES, EMB), dtype=jnp.float32)
        edge_index = jax.random.randint(ks[1], (2, 50000), 0, N_NODES, dtype=jnp.int64)
        s1 = 1.0 / np.sqrt(EMB)
        W1 = jax.random.normal(ks[2], (EMB, HEADS, F1), dtype=jnp.float32) * s1
        a_src1 = jax.random.normal(ks[3], (HEADS, F1), dtype=jnp.float32) * s1
        a_dst1 = jax.random.normal(ks[4], (HEADS, F1), dtype=jnp.float32) * s1
        b1 = jnp.zeros((HEADS * F1,), dtype=jnp.float32)
        W2 = jax.random.normal(ks[5], (EMB, 1, EMB), dtype=jnp.float32) * s1
        a_src2 = jax.random.normal(ks[6], (1, EMB), dtype=jnp.float32) * s1
        a_dst2 = jax.random.normal(ks[7], (1, EMB), dtype=jnp.float32) * s1
        b2 = jnp.zeros((EMB,), dtype=jnp.float32)
        return {'x': x, 'edge_index': edge_index, 'W1': W1, 'a_src1': a_src1, 'a_dst1': a_dst1, 'b1': b1, 'W2': W2, 'a_src2': a_src2, 'a_dst2': a_dst2, 'b2': b2}
    _L2_gnn_all = _L2_gnn_setup()
    _L2_gnn_in = {k: v for k, v in _L2_gnn_all.items() if k in ('W1', 'a_src1', 'a_dst1', 'b1', 'W2', 'a_src2', 'a_dst2', 'b2')}
    del _L2_gnn_all

    def _L2_ffn_setup():
        import jax, jax.numpy as jnp
        import numpy as np
        B, N, D = (16, 256, 256)
        NUM_EXPERTS, TOP_K, HEADS = (4, 2, 4)
        N_EDGES = 65536
        LN_EPS = 1e-05

        def _layernorm(x, g, b):
            mu = x.mean(-1, keepdims=True)
            var = ((x - mu) ** 2).mean(-1, keepdims=True)
            return (x - mu) * jax.lax.rsqrt(var + LN_EPS) * g + b

        def _forward(x, edge_index, W_gat, att_src, att_dst, b_gat, ln_gamma, ln_beta, W1, b1, W2, b2):
            Bc, Nc, Dc = x.shape
            M = Bc * Nc
            x_flat = x.reshape(M, Dc)
            h = (x_flat @ W_gat).reshape(M, HEADS, NUM_EXPERTS)
            loops = jnp.arange(M, dtype=edge_index.dtype)
            src = jnp.concatenate([edge_index[0], loops])
            dst = jnp.concatenate([edge_index[1], loops])
            a_src = (h * att_src).sum(-1)
            a_dst = (h * att_dst).sum(-1)
            e = jax.nn.leaky_relu(a_src[src] + a_dst[dst], negative_slope=0.2)
            e_max = jax.ops.segment_max(e, dst, num_segments=M)
            ee = jnp.exp(e - e_max[dst])
            denom = jax.ops.segment_sum(ee, dst, num_segments=M)
            alpha = ee / (denom[dst] + 1e-16)
            msg = h[src] * alpha[:, :, None]
            agg = jax.ops.segment_sum(msg, dst, num_segments=M).reshape(M, HEADS * NUM_EXPERTS) + b_gat
            scores = _layernorm(agg, ln_gamma, ln_beta).reshape(M, HEADS, NUM_EXPERTS).mean(1)
            scores = scores.reshape(Bc, Nc, NUM_EXPERTS)
            topk_s, topk_i = jax.lax.top_k(scores, TOP_K)
            w = jax.nn.softmax(topk_s, axis=-1)
            out = jnp.zeros_like(x)
            for ei in range(NUM_EXPERTS):
                g = jnp.where(topk_i == ei, w, 0.0).sum(-1)
                hh = jax.nn.gelu(x @ W1[ei] + b1[ei], approximate=False)
                out = out + g[..., None] * (hh @ W2[ei] + b2[ei])
            return out
        key = jax.random.key(seed)
        ks = jax.random.split(key, 8)
        s = 0.05
        return {'x': jax.random.normal(ks[0], (B, N, D), jnp.float32), 'W_gat': jax.random.normal(ks[1], (D, HEADS * NUM_EXPERTS), jnp.float32) * s, 'att_src': jax.random.normal(ks[2], (HEADS, NUM_EXPERTS), jnp.float32) * s, 'att_dst': jax.random.normal(ks[3], (HEADS, NUM_EXPERTS), jnp.float32) * s, 'b_gat': jnp.zeros((HEADS * NUM_EXPERTS,), jnp.float32), 'ln_gamma': jnp.ones((HEADS * NUM_EXPERTS,), jnp.float32), 'ln_beta': jnp.zeros((HEADS * NUM_EXPERTS,), jnp.float32), 'W1': jax.random.normal(ks[4], (NUM_EXPERTS, D, 2 * D), jnp.float32) * s, 'b1': jnp.zeros((NUM_EXPERTS, 2 * D), jnp.float32), 'W2': jax.random.normal(ks[5], (NUM_EXPERTS, 2 * D, D), jnp.float32) * s, 'b2': jnp.zeros((NUM_EXPERTS, D), jnp.float32), 'edge_index': jax.random.randint(ks[6], (2, N_EDGES), 0, B * N, jnp.int32)}
    _L2_ffn_all = _L2_ffn_setup()
    _L2_ffn_in = {k: v for k, v in _L2_ffn_all.items() if k in ('W_gat', 'att_src', 'att_dst', 'b_gat', 'ln_gamma', 'ln_beta', 'W1', 'b1', 'W2', 'b2', 'edge_index')}
    del _L2_ffn_all

    def _L3_gnn_setup():
        import jax, jax.numpy as jnp
        import numpy as np
        N, E, D = (1250, 20000, 256)
        H, C = (8, 32)
        key = jax.random.key(seed)
        ks = jax.random.split(key, 12)
        s = 1.0 / np.sqrt(D)
        return {'x': jax.random.normal(ks[0], (N, D), jnp.float32), 'edge_index': jax.random.randint(ks[1], (2, E), 0, N, jnp.int64), 'edge_attr': jax.random.normal(ks[2], (E, D), jnp.float32), 'Wq': jax.random.normal(ks[3], (D, H * C), jnp.float32) * s, 'bq': jnp.zeros((H * C,), jnp.float32), 'Wk': jax.random.normal(ks[4], (D, H * C), jnp.float32) * s, 'bk': jnp.zeros((H * C,), jnp.float32), 'Wv': jax.random.normal(ks[5], (D, H * C), jnp.float32) * s, 'bv': jnp.zeros((H * C,), jnp.float32), 'We': jax.random.normal(ks[6], (D, H * C), jnp.float32) * s, 'Ws': jax.random.normal(ks[7], (D, H * C), jnp.float32) * s, 'bs': jnp.zeros((H * C,), jnp.float32)}
    _L3_gnn_all = _L3_gnn_setup()
    _L3_gnn_in = {k: v for k, v in _L3_gnn_all.items() if k in ('Wq', 'bq', 'Wk', 'bk', 'Wv', 'bv', 'We', 'Ws', 'bs')}
    del _L3_gnn_all

    def _L3_ffn_setup():
        import jax, jax.numpy as jnp
        import numpy as np
        BN_EPS = 0.001

        def _bn(h, g, b, m, v):
            return g * (h - m) * jax.lax.rsqrt(v + BN_EPS) + b
        key = jax.random.key(seed)
        ks = jax.random.split(key, 8)
        B, F, Df = (256, 64, 256)
        E, H, D = (8, 256, 256)
        s1 = 1.0 / np.sqrt(Df)
        s2 = 1.0 / np.sqrt(H)
        return {'x': jax.random.normal(ks[0], (B, F, Df), jnp.float32), 'Wr': jax.random.normal(ks[1], (Df, E), jnp.float32) * s1, 'br': jnp.zeros((E,), jnp.float32), 'W1': jax.random.normal(ks[2], (E, Df, H), jnp.float32) * s1, 'b1': jnp.zeros((E, H), jnp.float32), 'g1': jnp.ones((E, H), jnp.float32), 'be1': jnp.zeros((E, H), jnp.float32), 'm1': jnp.zeros((E, H), jnp.float32), 'v1': jnp.ones((E, H), jnp.float32), 'W2': jax.random.normal(ks[3], (E, H, H), jnp.float32) * s2, 'b2': jnp.zeros((E, H), jnp.float32), 'g2': jnp.ones((E, H), jnp.float32), 'be2': jnp.zeros((E, H), jnp.float32), 'm2': jnp.zeros((E, H), jnp.float32), 'v2': jnp.ones((E, H), jnp.float32), 'Wo': jax.random.normal(ks[4], (E, H, D), jnp.float32) * s2, 'bo': jnp.zeros((E, D), jnp.float32)}
    _L3_ffn_all = _L3_ffn_setup()
    _L3_ffn_in = {k: v for k, v in _L3_ffn_all.items() if k in ('Wr', 'br', 'W1', 'b1', 'g1', 'be1', 'm1', 'v1', 'W2', 'b2', 'g2', 'be2', 'm2', 'v2', 'Wo', 'bo')}
    del _L3_ffn_all
    return {'x': x, 'src': src, 'dst': dst, 'edge_attr_256': edge_attr_256, 'L0_gnn_W': _L0_gnn_in['W'], 'L0_gnn_att_src': _L0_gnn_in['att_src'], 'L0_gnn_att_dst': _L0_gnn_in['att_dst'], 'L0_gnn_bias': _L0_gnn_in['bias'], 'L0_ffn_gate_w': _L0_ffn_in['gate_w'], 'L0_ffn_gate_b': _L0_ffn_in['gate_b'], 'L0_ffn_w1': _L0_ffn_in['w1'], 'L0_ffn_b1': _L0_ffn_in['b1'], 'L0_ffn_w2': _L0_ffn_in['w2'], 'L0_ffn_b2': _L0_ffn_in['b2'], 'L0_ffn_gamma': _L0_ffn_in['gamma'], 'L0_ffn_beta': _L0_ffn_in['beta'], 'L1_gnn_W': _L1_gnn_in['W'], 'L1_gnn_a_src': _L1_gnn_in['a_src'], 'L1_gnn_a_dst': _L1_gnn_in['a_dst'], 'L1_ffn_Wr': _L1_ffn_in['Wr'], 'L1_ffn_br': _L1_ffn_in['br'], 'L1_ffn_W1': _L1_ffn_in['W1'], 'L1_ffn_b1': _L1_ffn_in['b1'], 'L1_ffn_W2': _L1_ffn_in['W2'], 'L1_ffn_b2': _L1_ffn_in['b2'], 'L1_ffn_gamma': _L1_ffn_in['gamma'], 'L1_ffn_beta': _L1_ffn_in['beta'], 'L2_gnn_W1': _L2_gnn_in['W1'], 'L2_gnn_a_src1': _L2_gnn_in['a_src1'], 'L2_gnn_a_dst1': _L2_gnn_in['a_dst1'], 'L2_gnn_b1': _L2_gnn_in['b1'], 'L2_gnn_W2': _L2_gnn_in['W2'], 'L2_gnn_a_src2': _L2_gnn_in['a_src2'], 'L2_gnn_a_dst2': _L2_gnn_in['a_dst2'], 'L2_gnn_b2': _L2_gnn_in['b2'], 'L2_ffn_W_gat': _L2_ffn_in['W_gat'], 'L2_ffn_att_src': _L2_ffn_in['att_src'], 'L2_ffn_att_dst': _L2_ffn_in['att_dst'], 'L2_ffn_b_gat': _L2_ffn_in['b_gat'], 'L2_ffn_ln_gamma': _L2_ffn_in['ln_gamma'], 'L2_ffn_ln_beta': _L2_ffn_in['ln_beta'], 'L2_ffn_W1': _L2_ffn_in['W1'], 'L2_ffn_b1': _L2_ffn_in['b1'], 'L2_ffn_W2': _L2_ffn_in['W2'], 'L2_ffn_b2': _L2_ffn_in['b2'], 'L2_ffn_edge_index': _L2_ffn_in['edge_index'], 'L3_gnn_Wq': _L3_gnn_in['Wq'], 'L3_gnn_bq': _L3_gnn_in['bq'], 'L3_gnn_Wk': _L3_gnn_in['Wk'], 'L3_gnn_bk': _L3_gnn_in['bk'], 'L3_gnn_Wv': _L3_gnn_in['Wv'], 'L3_gnn_bv': _L3_gnn_in['bv'], 'L3_gnn_We': _L3_gnn_in['We'], 'L3_gnn_Ws': _L3_gnn_in['Ws'], 'L3_gnn_bs': _L3_gnn_in['bs'], 'L3_ffn_Wr': _L3_ffn_in['Wr'], 'L3_ffn_br': _L3_ffn_in['br'], 'L3_ffn_W1': _L3_ffn_in['W1'], 'L3_ffn_b1': _L3_ffn_in['b1'], 'L3_ffn_g1': _L3_ffn_in['g1'], 'L3_ffn_be1': _L3_ffn_in['be1'], 'L3_ffn_m1': _L3_ffn_in['m1'], 'L3_ffn_v1': _L3_ffn_in['v1'], 'L3_ffn_W2': _L3_ffn_in['W2'], 'L3_ffn_b2': _L3_ffn_in['b2'], 'L3_ffn_g2': _L3_ffn_in['g2'], 'L3_ffn_be2': _L3_ffn_in['be2'], 'L3_ffn_m2': _L3_ffn_in['m2'], 'L3_ffn_v2': _L3_ffn_in['v2'], 'L3_ffn_Wo': _L3_ffn_in['Wo'], 'L3_ffn_bo': _L3_ffn_in['bo']}

def reference(x, src, dst, edge_attr_256, L0_gnn_W, L0_gnn_att_src, L0_gnn_att_dst, L0_gnn_bias, L0_ffn_gate_w, L0_ffn_gate_b, L0_ffn_w1, L0_ffn_b1, L0_ffn_w2, L0_ffn_b2, L0_ffn_gamma, L0_ffn_beta, L1_gnn_W, L1_gnn_a_src, L1_gnn_a_dst, L1_ffn_Wr, L1_ffn_br, L1_ffn_W1, L1_ffn_b1, L1_ffn_W2, L1_ffn_b2, L1_ffn_gamma, L1_ffn_beta, L2_gnn_W1, L2_gnn_a_src1, L2_gnn_a_dst1, L2_gnn_b1, L2_gnn_W2, L2_gnn_a_src2, L2_gnn_a_dst2, L2_gnn_b2, L2_ffn_W_gat, L2_ffn_att_src, L2_ffn_att_dst, L2_ffn_b_gat, L2_ffn_ln_gamma, L2_ffn_ln_beta, L2_ffn_W1, L2_ffn_b1, L2_ffn_W2, L2_ffn_b2, L2_ffn_edge_index, L3_gnn_Wq, L3_gnn_bq, L3_gnn_Wk, L3_gnn_bk, L3_gnn_Wv, L3_gnn_bv, L3_gnn_We, L3_gnn_Ws, L3_gnn_bs, L3_ffn_Wr, L3_ffn_br, L3_ffn_W1, L3_ffn_b1, L3_ffn_g1, L3_ffn_be1, L3_ffn_m1, L3_ffn_v1, L3_ffn_W2, L3_ffn_b2, L3_ffn_g2, L3_ffn_be2, L3_ffn_m2, L3_ffn_v2, L3_ffn_Wo, L3_ffn_bo):
    import jax
    import jax.numpy as jnp

    def _L0_gnn_ref(x, edge_index, W, att_src, att_dst, bias):
        import jax, jax.numpy as jnp
        import numpy as np
        N_NODES = 3125
        N_EDGES = 100000
        H_SIZE = 256
        HEADS = 8
        HEAD_DIM = H_SIZE // HEADS
        NEG_SLOPE = 0.2
        'GATConv (concat heads) -> relu -> dropout(eval=identity).\n\n            x: [N, F]; edge_index: [2, E] with (src=row0, dst=row1) meaning message j->i.\n            '
        N = x.shape[0]
        h = jnp.einsum('nf,fhd->nhd', x, W)
        a_src = jnp.sum(h * att_src, axis=-1)
        a_dst = jnp.sum(h * att_dst, axis=-1)
        src = edge_index[0]
        dst = edge_index[1]
        e = jax.nn.leaky_relu(a_src[src] + a_dst[dst], NEG_SLOPE)
        e_max = jax.ops.segment_max(e, dst, num_segments=N)
        e_exp = jnp.exp(e - e_max[dst])
        denom = jax.ops.segment_sum(e_exp, dst, num_segments=N)
        alpha = e_exp / (denom[dst] + 1e-16)
        msg = h[src] * alpha[:, :, None]
        out = jax.ops.segment_sum(msg, dst, num_segments=N)
        out = out.reshape(N, -1) + bias
        return jax.nn.relu(out)

    def _L0_ffn_ref(x, gate_w, gate_b, w1, b1, w2, b2, gamma, beta):
        import jax, jax.numpy as jnp
        import numpy as np
        B, S, H, F, E, K = (8, 256, 256, 512, 16, 2)
        EPS = 1e-05
        gate_logits = x @ gate_w + gate_b
        topk_vals, topk_idx = jax.lax.top_k(gate_logits, K)
        topk_w = jax.nn.softmax(topk_vals, axis=-1)
        h = jax.nn.relu(jnp.einsum('bsh,ehf->bsef', x, w1) + b1)
        expert_out = jnp.einsum('bsef,efh->bseh', h, w2) + b2
        sel = jnp.take_along_axis(expert_out, topk_idx[:, :, :, None], axis=2)
        moe = jnp.sum(topk_w[..., None] * sel, axis=2)
        y = x + moe
        mu = jnp.mean(y, axis=-1, keepdims=True)
        var = jnp.var(y, axis=-1, keepdims=True)
        return (y - mu) / jnp.sqrt(var + EPS) * gamma + beta

    def _L1_gnn_ref(x, edge_index, W, a_src, a_dst):
        import jax, jax.numpy as jnp
        import numpy as np
        NEG_SLOPE = 0.2
        EPS = 1e-08
        N, E, IN_F, OUT_F, H = (3125, 50000, 256, 32, 8)
        num_nodes = x.shape[0]
        src, dst = (edge_index[0], edge_index[1])
        h = jnp.einsum('ni,hif->hnf', x, W)
        s_src = jnp.einsum('hnf,hf->hn', h, a_src)
        s_dst = jnp.einsum('hnf,hf->hn', h, a_dst)
        ea = (s_src[:, src] + s_dst[:, dst]).T
        ea = jnp.where(ea > 0, ea, NEG_SLOPE * ea)
        m = jax.ops.segment_max(ea, dst, num_segments=num_nodes)
        ea = jnp.exp(ea - m[dst])
        s = jax.ops.segment_sum(ea, dst, num_segments=num_nodes)
        ea = ea / (s[dst] + EPS)
        hn = jnp.transpose(h, (1, 0, 2))
        wf = hn[src] * ea[:, :, None]
        out = jax.ops.segment_sum(wf, dst, num_segments=num_nodes)
        return out.reshape(num_nodes, -1)

    def _L1_ffn_ref(x, Wr, br, W1, b1, W2, b2, gamma, beta):
        import math
        import jax, jax.numpy as jnp
        import numpy as np
        CAPACITY_FACTOR = 1.25
        TOP_K = 2
        LN_EPS = 1e-05

        def _layer_norm(x, gamma, beta):
            mu = jnp.mean(x, axis=-1, keepdims=True)
            var = jnp.var(x, axis=-1, keepdims=True)
            return (x - mu) * jax.lax.rsqrt(var + LN_EPS) * gamma + beta
        B, S, D = x.shape
        E = Wr.shape[1]
        N = B * S
        K = TOP_K
        logits = jnp.mean(x, axis=1) @ Wr + br
        routing_weights = jax.nn.softmax(logits, axis=-1)
        capacity = float(math.ceil(N * CAPACITY_FACTOR / E))
        expected_loads = routing_weights.sum(axis=0) * (N / B)
        scale = jnp.where(expected_loads > capacity, capacity / expected_loads, 1.0)
        routing_weights = jax.nn.softmax(routing_weights * scale, axis=-1)
        rw_tok = jnp.broadcast_to(routing_weights[:, None, :], (B, S, E)).reshape(N, E)
        top_w, top_i = jax.lax.top_k(rw_tok, K)
        top_w = jax.nn.softmax(top_w, axis=-1)
        xf = x.reshape(N, D)
        h = jax.nn.gelu(jnp.einsum('nd,edf->enf', xf, W1) + b1[:, None, :], approximate=False)
        y = jnp.einsum('enf,efd->end', h, W2) + b2[:, None, :]
        w_dense = jnp.zeros((N, E), x.dtype).at[jnp.arange(N)[:, None], top_i].add(top_w)
        out = jnp.einsum('ne,end->nd', w_dense, y).reshape(B, S, D)
        out = _layer_norm(out + x, gamma, beta)
        return out

    def _L2_gnn_ref(x, edge_index, W1, a_src1, a_dst1, b1, W2, a_src2, a_dst2, b2):
        import jax, jax.numpy as jnp
        import numpy as np
        N_NODES = 3125
        EMB = 256
        HEADS = 8
        NEG_SLOPE = 0.2

        def gat_conv(x, src, dst, W, a_src, a_dst, b, num_nodes):
            h = jnp.einsum('nd,dhf->nhf', x, W)
            al_s = jnp.sum(h * a_src, axis=-1)
            al_d = jnp.sum(h * a_dst, axis=-1)
            logits = jax.nn.leaky_relu(al_s[src] + al_d[dst], NEG_SLOPE)
            m = jax.ops.segment_max(logits, dst, num_segments=num_nodes)
            e = jnp.exp(logits - m[dst])
            z = jax.ops.segment_sum(e, dst, num_segments=num_nodes)
            alpha = e / (z[dst] + 1e-16)
            msg = h[src] * alpha[..., None]
            out = jax.ops.segment_sum(msg, dst, num_segments=num_nodes)
            return out.reshape(num_nodes, -1) + b
        n = x.shape[0]
        loops = jnp.arange(n, dtype=edge_index.dtype)
        src = jnp.concatenate([edge_index[0], loops])
        dst = jnp.concatenate([edge_index[1], loops])
        h = gat_conv(x, src, dst, W1, a_src1, a_dst1, b1, n)
        out = gat_conv(h, src, dst, W2, a_src2, a_dst2, b2, n)
        return out

    def _L2_ffn_ref(x, W_gat, att_src, att_dst, b_gat, ln_gamma, ln_beta, W1, b1, W2, b2, edge_index):
        import jax, jax.numpy as jnp
        import numpy as np
        B, N, D = (16, 256, 256)
        NUM_EXPERTS, TOP_K, HEADS = (4, 2, 4)
        N_EDGES = 65536
        LN_EPS = 1e-05

        def _layernorm(x, g, b):
            mu = x.mean(-1, keepdims=True)
            var = ((x - mu) ** 2).mean(-1, keepdims=True)
            return (x - mu) * jax.lax.rsqrt(var + LN_EPS) * g + b

        def _forward(x, edge_index, W_gat, att_src, att_dst, b_gat, ln_gamma, ln_beta, W1, b1, W2, b2):
            Bc, Nc, Dc = x.shape
            M = Bc * Nc
            x_flat = x.reshape(M, Dc)
            h = (x_flat @ W_gat).reshape(M, HEADS, NUM_EXPERTS)
            loops = jnp.arange(M, dtype=edge_index.dtype)
            src = jnp.concatenate([edge_index[0], loops])
            dst = jnp.concatenate([edge_index[1], loops])
            a_src = (h * att_src).sum(-1)
            a_dst = (h * att_dst).sum(-1)
            e = jax.nn.leaky_relu(a_src[src] + a_dst[dst], negative_slope=0.2)
            e_max = jax.ops.segment_max(e, dst, num_segments=M)
            ee = jnp.exp(e - e_max[dst])
            denom = jax.ops.segment_sum(ee, dst, num_segments=M)
            alpha = ee / (denom[dst] + 1e-16)
            msg = h[src] * alpha[:, :, None]
            agg = jax.ops.segment_sum(msg, dst, num_segments=M).reshape(M, HEADS * NUM_EXPERTS) + b_gat
            scores = _layernorm(agg, ln_gamma, ln_beta).reshape(M, HEADS, NUM_EXPERTS).mean(1)
            scores = scores.reshape(Bc, Nc, NUM_EXPERTS)
            topk_s, topk_i = jax.lax.top_k(scores, TOP_K)
            w = jax.nn.softmax(topk_s, axis=-1)
            out = jnp.zeros_like(x)
            for ei in range(NUM_EXPERTS):
                g = jnp.where(topk_i == ei, w, 0.0).sum(-1)
                hh = jax.nn.gelu(x @ W1[ei] + b1[ei], approximate=False)
                out = out + g[..., None] * (hh @ W2[ei] + b2[ei])
            return out
        return _forward(x, edge_index, W_gat, att_src, att_dst, b_gat, ln_gamma, ln_beta, W1, b1, W2, b2)

    def _L3_gnn_ref(x, edge_index, edge_attr, Wq, bq, Wk, bk, Wv, bv, We, Ws, bs):
        import jax, jax.numpy as jnp
        import numpy as np
        N, E, D = (1250, 20000, 256)
        H, C = (8, 32)
        n = x.shape[0]
        src, dst = (edge_index[0], edge_index[1])
        q = (x @ Wq + bq).reshape(n, H, C)
        k = (x @ Wk + bk).reshape(n, H, C)
        v = (x @ Wv + bv).reshape(n, H, C)
        e = (edge_attr @ We).reshape(-1, H, C)
        kj = k[src] + e
        alpha = jnp.einsum('ehc,ehc->eh', q[dst], kj) / jnp.sqrt(jnp.float32(C))
        amax = jax.ops.segment_max(alpha, dst, num_segments=n)
        ea = jnp.exp(alpha - amax[dst])
        denom = jax.ops.segment_sum(ea, dst, num_segments=n)
        alpha = ea / (denom[dst] + 1e-16)
        msg = (v[src] + e) * alpha[:, :, None]
        out = jax.ops.segment_sum(msg, dst, num_segments=n)
        out = out.reshape(n, H * C) + (x @ Ws + bs)
        return out

    def _L3_ffn_ref(x, Wr, br, W1, b1, g1, be1, m1, v1, W2, b2, g2, be2, m2, v2, Wo, bo):
        import jax, jax.numpy as jnp
        import numpy as np
        BN_EPS = 0.001

        def _bn(h, g, b, m, v):
            return g * (h - m) * jax.lax.rsqrt(v + BN_EPS) + b
        feat = jnp.mean(x, axis=0)
        w = jax.nn.softmax(feat @ Wr + br, axis=-1)
        h = jnp.einsum('bfd,edh->bfeh', x, W1) + b1
        h = jax.nn.relu(_bn(h, g1, be1, m1, v1))
        h = jnp.einsum('bfeh,ehk->bfek', h, W2) + b2
        h = jax.nn.relu(_bn(h, g2, be2, m2, v2))
        y = jnp.einsum('bfeh,ehd->bfed', h, Wo) + bo
        return jnp.einsum('bfed,fe->bfd', y, w)
    edge_index = jnp.stack([src, dst])
    x = x + _L0_gnn_ref(_layernorm(x, axis=-1), edge_index, L0_gnn_W, L0_gnn_att_src, L0_gnn_att_dst, L0_gnn_bias)
    x = x + _L0_ffn_ref(_layernorm(x, axis=-1)[None], L0_ffn_gate_w, L0_ffn_gate_b, L0_ffn_w1, L0_ffn_b1, L0_ffn_w2, L0_ffn_b2, L0_ffn_gamma, L0_ffn_beta)[0]
    x = x + _L1_gnn_ref(_layernorm(x, axis=-1), edge_index, L1_gnn_W, L1_gnn_a_src, L1_gnn_a_dst)
    x = x + _L1_ffn_ref(_layernorm(x, axis=-1)[None], L1_ffn_Wr, L1_ffn_br, L1_ffn_W1, L1_ffn_b1, L1_ffn_W2, L1_ffn_b2, L1_ffn_gamma, L1_ffn_beta)[0]
    x = x + _L2_gnn_ref(_layernorm(x, axis=-1), edge_index, L2_gnn_W1, L2_gnn_a_src1, L2_gnn_a_dst1, L2_gnn_b1, L2_gnn_W2, L2_gnn_a_src2, L2_gnn_a_dst2, L2_gnn_b2)
    x = x + _L2_ffn_ref(_layernorm(x, axis=-1)[None], L2_ffn_W_gat, L2_ffn_att_src, L2_ffn_att_dst, L2_ffn_b_gat, L2_ffn_ln_gamma, L2_ffn_ln_beta, L2_ffn_W1, L2_ffn_b1, L2_ffn_W2, L2_ffn_b2, L2_ffn_edge_index)[0]
    x = x + _L3_gnn_ref(_layernorm(x, axis=-1), edge_index, edge_attr_256, L3_gnn_Wq, L3_gnn_bq, L3_gnn_Wk, L3_gnn_bk, L3_gnn_Wv, L3_gnn_bv, L3_gnn_We, L3_gnn_Ws, L3_gnn_bs)
    x = x + _L3_ffn_ref(_layernorm(x, axis=-1)[None], L3_ffn_Wr, L3_ffn_br, L3_ffn_W1, L3_ffn_b1, L3_ffn_g1, L3_ffn_be1, L3_ffn_m1, L3_ffn_v1, L3_ffn_W2, L3_ffn_b2, L3_ffn_g2, L3_ffn_be2, L3_ffn_m2, L3_ffn_v2, L3_ffn_Wo, L3_ffn_bo)[0]
    return x

_drawn_inputs = setup_inputs


def setup_inputs(seed=0):
    import zlib

    import numpy as np

    out = dict(_drawn_inputs(seed))
    spreads = {'L0_gnn_bias': (0.0, 0.1),
     'L0_ffn_gate_b': (0.0, 0.1),
     'L0_ffn_b1': (0.0, 0.494),
     'L0_ffn_b2': (0.0, 0.1),
     'L0_ffn_gamma': (1.0, 0.2),
     'L0_ffn_beta': (0.0, 0.1),
     'L1_ffn_br': (0.0, 0.8),
     'L1_ffn_b1': (0.0, 0.416),
     'L1_ffn_b2': (0.0, 0.267),
     'L1_ffn_gamma': (1.0, 0.2),
     'L1_ffn_beta': (0.0, 0.1),
     'L2_gnn_b1': (0.0, 0.1),
     'L2_gnn_b2': (0.0, 0.1),
     'L2_ffn_b_gat': (0.0, 0.1),
     'L2_ffn_ln_gamma': (1.0, 0.2),
     'L2_ffn_ln_beta': (0.0, 0.481),
     'L2_ffn_b1': (0.0, 0.462),
     'L2_ffn_b2': (0.0, 0.346),
     'L3_gnn_bq': (0.0, 0.386),
     'L3_gnn_bk': (0.0, 2.0),
     'L3_gnn_bv': (0.0, 0.296),
     'L3_gnn_bs': (0.0, 0.303),
     'L3_ffn_br': (0.0, 0.8),
     'L3_ffn_b1': (0.0, 0.8),
     'L3_ffn_g1': (1.0, 0.6),
     'L3_ffn_be1': (0.0, 0.8),
     'L3_ffn_m1': (0.0, 0.8),
     'L3_ffn_v1': (1.0, 0.6),
     'L3_ffn_b2': (0.0, 0.747),
     'L3_ffn_g2': (1.0, 0.6),
     'L3_ffn_be2': (0.0, 0.779),
     'L3_ffn_m2': (0.0, 0.718),
     'L3_ffn_v2': (1.0, 0.6),
     'L3_ffn_bo': (0.0, 0.55)}
    factors = {'L1_ffn_Wr': 64.0,
     'L2_gnn_a_src1': 3.112,
     'L2_gnn_a_dst1': 8.0,
     'L2_gnn_a_src2': 4.876,
     'L2_gnn_a_dst2': 8.0,
     'L2_ffn_att_src': 3.05,
     'L2_ffn_att_dst': 4.517}
    for name, (base, spread) in spreads.items():
        noise = np.random.default_rng([zlib.crc32(name.encode()), seed]).standard_normal(out[name].shape)
        drawn = base * np.exp(spread * noise) if base else spread * noise
        out[name] = jnp.asarray(drawn.astype(out[name].dtype))
    for name, factor in factors.items():
        out[name] = (out[name] * factor).astype(out[name].dtype)
    return out
```

```python
import math
from contextlib import ExitStack

import numpy as np
import concourse.bass as bass
from concourse import mybir

F32 = mybir.dt.float32
BF16 = mybir.dt.bfloat16
I32 = mybir.dt.int32
U32 = mybir.dt.uint32
ALU = mybir.AluOpType
ACT = mybir.ActivationFunctionType
AX = mybir.AxisListType

P = 128
N_NODES = 3125
D = 256
DC = D // P
NT = -(-N_NODES // P)
NPAD = NT * P
LAST = N_NODES - (NT - 1) * P
N_EDGES = 50000
HEADS = 8
C = D // HEADS
ROW = D + HEADS

STEPS = (N_EDGES + NT * (P - 1)) // P + 1
BATCH = 8
SLOTS = 4
KK = P // HEADS
RUN = STEPS // KK
RUNE = RUN * P
NB = STEPS // BATCH
assert STEPS == 416 and STEPS % (BATCH * SLOTS) == 0 and STEPS % KK == 0
TAB = STEPS + BATCH
EPAD = (STEPS + NT + 2) * P
NEG = -1.0e30

UN = 5
assert NT % UN == 0


class Phase:

    def __init__(self, nc, name):
        self.nc, self.name, self.stack = nc, name, ExitStack()

    def __enter__(self):
        self.stack.__enter__()
        return self

    def __exit__(self, *a):
        return self.stack.__exit__(*a)

    def sb(self, name, shape, dt=F32):
        return self.stack.enter_context(self.nc.sbuf_tensor(f"{self.name}_{name}", shape, dt))

    def psum(self, name, shape, dt=F32):
        return self.stack.enter_context(self.nc.psum_tensor(f"{self.name}_{name}", shape, dt))

    def sem(self, name):
        return self.stack.enter_context(self.nc.semaphore(f"{self.name}_{name}"))


class Chain:

    def __init__(self, eng, sem):
        self.eng, self.sem, self.n = eng, sem, 0

    def link(self, ins):
        ins.then_inc(self.sem, 1)
        self.n += 1
        self.eng.wait_ge(self.sem, self.n)

    def note(self, ins):
        ins.then_inc(self.sem, 1)
        self.n += 1

    def settle(self):
        self.eng.wait_ge(self.sem, self.n)


def clear_semaphores(nc):
    given_back = list(nc.released_uncleared_semaphores)
    nc.gpsimd.dma_reset(range(min(given_back), max(given_back) + 1))
    nc.all_engine_barrier(sems_to_clear=range(min(given_back), max(given_back) + 1))


def bcast(ap, n):
    return ap.unsqueeze(len(ap.shape)).to_broadcast(list(ap.shape) + [n])


def over_partitions(ap, n=P):
    return ap.partition_broadcast(n)


def load_constants(nc, K, x_in):
    with Phase(nc, "const") as ph:
        ident_zero, ident_set, iota_set = ph.sem("ident_zero"), ph.sem("ident_set"), ph.sem("iota_set")
        x_zero, x_in_sem, conv = ph.sem("x_zero"), ph.sem("x_in"), ph.sem("conv")
        col_i = ph.sb("col_i", [P, P], I32)
        row_i = ph.sb("row_i", [P, 1], I32)
        with nc.Block() as block:
            @block.gpsimd
            def _(pool):
                nc.gpsimd.memset(K.ident[:], 0.0).then_inc(ident_zero, 1)
                pool.wait_ge(ident_zero, 1)
                nc.gpsimd.affine_select(out=K.ident[:], in_=K.ident[:], compare_op=ALU.not_equal, fill=1.0,
                                        base=0, pattern=[[-1, P]], channel_multiplier=1).then_inc(ident_set, 1)
                nc.gpsimd.iota(col_i[:], [[1, P]], base=0, channel_multiplier=0).then_inc(iota_set, 1)
                nc.gpsimd.iota(row_i[:], [[1, 1]], base=0, channel_multiplier=1).then_inc(iota_set, 1)
                nc.gpsimd.memset(K.izero[:], 0).then_inc(ident_set, 1)

            @block.vector
            def _(dve):
                nc.vector.memset(K.x[:, NT - 1, :], 0.0).then_inc(x_zero, 1)
                nc.vector.memset(K.ones[:], 1.0)
                dve.wait_ge(iota_set, 2)
                nc.vector.tensor_copy(K.col[:], col_i[:])
                nc.vector.tensor_copy(K.row[:], row_i[:])

            @block.sync
            def _(sp):
                full = (NT - 1) * P
                sp.dma_start(K.x[:, 0:NT - 1, :], x_in[0:full, :].rearrange("(t p) d -> p t d", p=P)).then_inc(x_in_sem, 16)
                sp.wait_ge(x_zero, 1)
                sp.dma_start(K.x[0:LAST, NT - 1, :], x_in[full:N_NODES, :]).then_inc(x_in_sem, 16)
                sp.wait_ge(x_in_sem, 32)


def edge_schedule(nc, K, src, dst):
    G4 = 4
    KP = STEPS // G4
    NCH, CH = 125, N_EDGES // 125
    SHIFTS = 7
    with Phase(nc, "sched") as ph:
        pad_d = [nc.dram_tensor(f"{s}_pad", (EPAD // P, P), I32, kind="Internal").ap() for s in ("src", "dst")]
        step_blk = nc.dram_tensor("step_blk", (1, STEPS), I32, kind="Internal").ap()
        keys_d = nc.dram_tensor("keys", (1, STEPS * P + 2), F32, kind="Internal").ap()

        spare = ph.sb("spare", [2, 2, (EPAD - N_EDGES) // 2], I32)
        d_i = ph.sb("d_i", [NCH, CH], I32)
        d_f = ph.sb("d_f", [NCH, CH])
        thr_i = ph.sb("thr_i", [P, NT], I32)
        thr = ph.sb("thr", [P, NT])
        below = ph.sb("below", [NCH, NT, CH])
        cnt_part = ph.sb("cnt_part", [NCH, NT])
        off = ph.sb("off", [P, NT + 1])
        cnt = ph.sb("cnt", [P, NT])
        nt_i = ph.sb("nt_i", [P, NT], I32)
        nt_s = ph.sb("nt_s", [P, NT], I32)
        nt_f = ph.sb("nt_f", [P, NT])
        one25 = ph.sb("one25", [P, NT])
        first_step = ph.sb("first_step", [P, NT])
        delta = ph.sb("delta", [P, NT])
        kio_i = ph.sb("kio_i", [KP, G4], I32)
        kio = ph.sb("kio", [KP, G4])
        passed = ph.sb("passed", [KP, G4, NT])
        part = ph.sb("part", [KP, G4, NT])
        blk = ph.sb("blk", [KP, G4])
        e0 = ph.sb("e0", [KP, G4])
        end = ph.sb("end", [KP, G4])
        tmp4 = ph.sb("tmp4", [KP, G4])
        blk_i = ph.sb("blk_i", [KP, G4], I32)
        e0_i = ph.sb("e0_i", [KP, G4], I32)
        line_i = ph.sb("line_i", [KP, G4], I32)
        line = ph.sb("line", [KP, G4, 2], U32)
        bit_i = ph.sb("bit_i", [KP, SHIFTS, G4], I32)
        bit = ph.sb("bit", [KP, SHIFTS, G4])
        lines_i = ph.sb("lines_i", [KP, G4, 2, 2, P], I32)
        lines = [ph.sb(f"lines{n}", [KP, G4, 2, 2 * P]) for n in range(2)]
        moved = ph.sb("moved", [KP, G4, 2, 2 * P])
        rows = ph.sb("rows", [KP, G4, 2, P])
        ids = ph.sb("ids", [KP, G4, P])
        valid = ph.sb("valid", [KP, G4, P])
        rel = ph.sb("rel", [KP, G4, P])
        rel1 = ph.sb("rel1", [KP, G4, P])
        rel_b = ph.sb("rel_b", [KP, G4, P], BF16)
        idc = ph.sb("idc", [KP, G4, P])
        bad = ph.sb("bad", [KP, G4, P])
        edge2 = ph.sb("edge2", [1, 2])
        keys = ph.sb("keys", [P, RUNE + 2])
        seg = ph.sb("seg", [P, 2])
        ps_last = [ph.psum(f"ps_last{n}", [P, 4, P]) for n in range(2)]
        seg_row = ph.sb("seg_row", [2, P])
        seg_row2 = ph.sb("seg_row2", [1, P])
        ps_off = ph.psum("ps_off", [P, NT])
        ps_tab = ph.psum("ps_tab", [P, STEPS])
        ps_seg = ph.psum("ps_seg", [P, P])

        pads, ld, made, dv, offs, rdy = (ph.sem(s) for s in ("pads", "ld", "made", "dv", "offs", "rdy"))
        stepd, row0, rows_in, keyw, keyin = (ph.sem(s) for s in ("stepd", "row0", "rows_in", "keyw", "keyin"))
        tab_ready, tab_done, tab_copied, kready = (ph.sem(s) for s in ("tab_ready", "tab_done", "tab_copied", "kready"))
        groups = [range(g, min(g + 4, RUN)) for g in range(0, RUN, 4)]
        last_t, last_kept = ph.sem("last_t"), ph.sem("last_kept")
        keys_made, seg_made, seg_t, relw, seg2, segw = (ph.sem(s) for s in ("keys_made", "seg_made", "seg_t", "relw", "seg2", "segw"))

        with nc.Block() as block:
            @block.gpsimd
            def _(pool):
                nc.gpsimd.memset(spare[:, 0, :], 0)
                nc.gpsimd.memset(spare[:, 1, :], -1).then_inc(made, 1)
                nc.gpsimd.iota(thr_i[:], [[P, NT]], base=P, channel_multiplier=0).then_inc(made, 1)
                nc.gpsimd.iota(kio_i[:], [[KP, G4]], base=0, channel_multiplier=1).then_inc(made, 1)
                nc.gpsimd.memset(edge2[:], -1.0).then_inc(made, 1)
                pool.wait_ge(pads, 64)
                pool.wait_ge(rdy, 1)
                for g in range(G4):
                    for a in range(2):
                        for n in range(2):
                            nc.gpsimd.indirect_dma_start(
                                out=lines_i[:, g, a, n, :], out_offset=None, in_=pad_d[a],
                                in_offset=bass.IndirectOffsetOnAxis(ap=line[:, g, n:n + 1], axis=0)).then_inc(rows_in, 16)

            @block.sync
            def _(sp):
                sp.dma_start(d_i[:], dst.rearrange("(p c) -> p c", c=CH)).then_inc(ld, 16)
                for a, edges in enumerate((src, dst)):
                    flat = pad_d[a].rearrange("r e -> (r e)")
                    sp.dma_start(flat[0:N_EDGES], edges).then_inc(pads, 16)
                sp.wait_ge(made, 4)
                for a in range(2):
                    flat = pad_d[a].rearrange("r e -> (r e)")
                    sp.dma_start(flat[N_EDGES:EPAD].rearrange("(a n) -> a n", a=2), spare[:, a, :]).then_inc(pads, 16)
                sp.dma_start(keys_d[:, 0:1], edge2[:, 0:1]).then_inc(keyw, 16)
                sp.dma_start(keys_d[:, STEPS * P + 1:STEPS * P + 2], edge2[:, 1:2]).then_inc(keyw, 16)
                sp.wait_ge(rdy, 1)
                sp.dma_start(step_blk.rearrange("o (g p) -> p (o g)", p=KP), blk_i[:]).then_inc(stepd, 16)
                sp.wait_ge(stepd, 16)
                sp.dma_start(K.blk_row[:], step_blk).then_inc(row0, 16)
                sp.wait_ge(row0, 16)
                sp.wait_ge(kready, 1)
                sp.dma_start(keys_d[0, 1:1 + STEPS * P].rearrange("(g p e) -> p g e", p=KP, e=P), rows[:, :, 1, :]).then_inc(keyw, 16)
                sp.dma_start(K.rel_rows.rearrange("(g p) e -> p g e", p=KP), rel_b[:]).then_inc(relw, 16)
                sp.wait_ge(keyw, 48)
                for kk in range(KK):
                    sp.dma_start(keys[kk * HEADS:(kk + 1) * HEADS, :],
                                 over_partitions(keys_d[0, kk * RUNE:kk * RUNE + RUNE + 2], HEADS)).then_inc(keyin, 16)
                sp.wait_ge(relw, 16)

            @block.vector
            def _(dve):
                ch = Chain(dve, dv)
                dve.wait_ge(made, 4)
                ch.note(nc.vector.tensor_copy(thr[:], thr_i[:]))
                ch.note(nc.vector.tensor_copy(kio[:], kio_i[:]))
                ch.note(nc.vector.memset(one25[:], 1.0))
                ch.note(nc.vector.memset(off[:, 0:1], 0.0))
                dve.wait_ge(ld, 16)
                ch.link(nc.vector.tensor_copy(d_f[:], d_i[:]))
                ch.link(nc.vector.tensor_tensor(below[:], d_f[:].unsqueeze(1).to_broadcast([NCH, NT, CH]),
                                                bcast(thr[0:NCH, :], CH), ALU.is_lt))
                nc.vector.tensor_reduce(cnt_part[:], below[:], AX.X, ALU.add).then_inc(offs, 1)
                dve.wait_ge(tab_done, 1)
                ch.link(nc.vector.tensor_copy(off[:, 1:NT + 1], ps_off[:]))
                ch.link(nc.vector.tensor_tensor(cnt[:], off[:, 1:NT + 1], off[:, 0:NT], ALU.subtract))
                ch.link(nc.vector.tensor_scalar(nt_i[:], cnt[:], float(P - 1), None, ALU.add))
                ch.link(nc.vector.tensor_scalar(nt_s[:], nt_i[:], 7, None, ALU.arith_shift_right))
                ch.link(nc.vector.tensor_copy(nt_f[:], nt_s[:]))
                ch.note(nc.vector.tensor_tensor_scan(first_step[:], one25[:], nt_f[:], 0.0, ALU.mult, ALU.add))
                ch.link(nc.vector.scalar_tensor_tensor(delta[:], nt_f[:], -float(P), cnt[:], ALU.mult, ALU.add))
                ch.link(nc.vector.tensor_tensor(passed[:], bcast(kio[:], NT),
                                                first_step[0:KP, :].unsqueeze(1).to_broadcast([KP, G4, NT]), ALU.is_ge))
                ch.note(nc.vector.tensor_reduce(blk[:], passed[:], AX.X, ALU.add))
                ch.link(nc.vector.tensor_tensor(part[:], passed[:], delta[0:KP, :].unsqueeze(1).to_broadcast([KP, G4, NT]), ALU.mult))
                ch.link(nc.vector.tensor_reduce(tmp4[:], part[:], AX.X, ALU.add))
                ch.note(nc.vector.scalar_tensor_tensor(e0[:], kio[:], float(P), tmp4[:], ALU.mult, ALU.add))
                ch.link(nc.vector.tensor_tensor(part[:, :, 0:NT - 1], passed[:, :, 0:NT - 1],
                                                cnt[0:KP, 1:NT].unsqueeze(1).to_broadcast([KP, G4, NT - 1]), ALU.mult))
                ch.link(nc.vector.tensor_reduce(tmp4[:], part[:, :, 0:NT - 1], AX.X, ALU.add))
                ch.note(nc.vector.tensor_scalar(end[:], tmp4[:], cnt[0:KP, 0:1], None, ALU.add))
                ch.settle()
                ch.note(nc.vector.tensor_copy(blk_i[:], blk[:]))
                ch.link(nc.vector.tensor_copy(e0_i[:], e0[:]))
                ch.link(nc.vector.tensor_scalar(line_i[:], e0_i[:], 7, None, ALU.arith_shift_right))
                ch.note(nc.vector.tensor_copy(line[:, :, 0], line_i[:]))
                ch.link(nc.vector.tensor_scalar(line[:, :, 1], line_i[:], 1.0, None, ALU.add))
                dve.sem_inc(rdy, 1)
                for n in range(SHIFTS):
                    ch.note(nc.vector.tensor_scalar(bit_i[:, n, :], e0_i[:], n, 1, ALU.arith_shift_right, ALU.bitwise_and))
                ch.settle()
                ch.note(nc.vector.tensor_copy(bit[:], bit_i[:]))
                dve.wait_ge(rows_in, 16 * 4 * G4)
                ch.link(nc.vector.tensor_copy(lines[0][:].rearrange("p g a (n e) -> p g a n e", e=P), lines_i[:]))
                width = 2 * P
                for n in reversed(range(SHIFTS)):
                    was, now = lines[n % 2], lines[(n + 1) % 2]
                    width -= 1 << n
                    for g in range(G4):
                        ch.note(nc.vector.tensor_tensor(moved[:, g, :, 0:width], was[:, g, :, (1 << n):(1 << n) + width], was[:, g, :, 0:width], ALU.subtract))
                    ch.settle()
                    for g in range(G4):
                        ch.note(nc.vector.scalar_tensor_tensor(now[:, g, :, 0:width], moved[:, g, :, 0:width], bit[:, n, g:g + 1],
                                                               was[:, g, :, 0:width], ALU.mult, ALU.add))
                    ch.settle()
                ch.link(nc.vector.tensor_copy(rows[:], lines[1][:, :, :, 0:P]))
                ch.link(nc.vector.tensor_tensor(ids[:], K.col[0:KP, :].unsqueeze(1).to_broadcast([KP, G4, P]), bcast(e0[:], P), ALU.add))
                ch.note(nc.vector.tensor_scalar(idc[:], ids[:], float(N_EDGES - 1), None, ALU.min))
                ch.note(nc.vector.tensor_tensor(valid[:], ids[:], bcast(end[:], P), ALU.is_lt))
                ch.note(nc.vector.tensor_scalar(tmp4[:], blk[:], -float(P), 1.0, ALU.mult, ALU.add))
                ch.settle()
                ch.link(nc.vector.tensor_tensor(rel[:], rows[:, :, 1, :], bcast(tmp4[:], P), ALU.add))
                ch.link(nc.vector.tensor_tensor(rel1[:], rel[:], valid[:], ALU.mult))
                ch.link(nc.vector.tensor_scalar(rel[:], rel1[:], 1.0, None, ALU.subtract))
                ch.note(nc.vector.tensor_copy(rel_b[:], rel[:]))
                ch.note(nc.vector.tensor_scalar(bad[:], valid[:], 1.0, -NEG, ALU.subtract, ALU.mult))
                ch.settle()
                dve.sem_inc(kready, 1)
                ch.note(nc.vector.memset(K.src_t[:, STEPS:TAB], 0))
                ch.note(nc.vector.memset(K.id_t[:, STEPS:TAB], 0))
                for n, to in enumerate((K.rel_t, K.bad_t, K.src_t, K.id_t)):
                    dve.wait_ge(tab_done, 2 + n)
                    nc.vector.tensor_copy(to[:, 0:STEPS], ps_tab[:]).then_inc(tab_copied, 1)
                dve.wait_ge(keyin, 16 * KK)
                ch.note(nc.vector.tensor_tensor(K.mask_f[:], keys[:, 1:RUNE + 1], keys[:, 0:RUNE], ALU.not_equal))
                ch.link(nc.vector.tensor_tensor(K.mask_r[:], keys[:, 1:RUNE + 1], keys[:, 2:RUNE + 2], ALU.not_equal))
                ch.note(nc.vector.tensor_scalar(K.mask_f[:], K.mask_f[:], NEG, None, ALU.mult))
                ch.link(nc.vector.tensor_scalar(K.mask_r[:], K.mask_r[:], NEG, None, ALU.mult))
                nc.vector.tensor_reduce(seg[:, 0:1], K.mask_f[:], AX.X, ALU.min).then_inc(seg_made, 1)
                nc.vector.tensor_reduce(seg[:, 1:2], K.mask_r[:], AX.X, ALU.min).then_inc(seg_made, 1)
                for a, to in ((0, K.cut_f), (1, K.cut_r)):
                    dve.wait_ge(seg_t, a + 1)
                    ch.link(nc.vector.tensor_copy(to[:].rearrange("o (h k) -> o h k", h=HEADS),
                                                  ps_seg[0:1, :].rearrange("o (k h) -> o h k", h=HEADS)))
                    edge = 0 if a == 0 else KK - 1
                    ch.link(nc.vector.memset(to[:].rearrange("o (h k) -> o h k", h=HEADS)[:, :, edge], NEG))
                    dve.sem_inc(segw, 1)
                for q, gs in enumerate(groups):
                    dve.wait_ge(last_t, q + 1)
                    nc.vector.tensor_scalar(K.last_t[:].rearrange("p (k g) -> p g k", g=RUN)[:, gs[0]:gs[-1] + 1],
                                            ps_last[q % 2][:, 0:len(gs)].rearrange("p g (k h) -> p g k h", h=HEADS)[:, :, :, 0],
                                            1.0 / NEG, None, ALU.mult).then_inc(last_kept, 1)

            @block.tensor
            def _(pe):
                pe.wait_ge(offs, 1)
                nc.tensor.matmul(ps_off[:], K.ones[0:NCH, :], cnt_part[:], start=True, stop=True).then_inc(tab_done, 1)
                pe.wait_ge(kready, 1)
                for n, frm in enumerate((rel, bad, None, idc)):
                    if n:
                        pe.wait_ge(tab_copied, n)
                    for g in range(G4):
                        rows_of = rows[:, g, 0, :] if frm is None else frm[:, g, :]
                        last = nc.tensor.transpose(ps_tab[:, g * KP:(g + 1) * KP], rows_of, K.ident[0:KP, 0:KP])
                    last.then_inc(tab_done, 1)
                pe.wait_ge(seg_made, 2)
                for a in range(2):
                    if a:
                        pe.wait_ge(segw, 1)
                    nc.tensor.transpose(ps_seg[0:1, :], seg[:, a:a + 1], K.ident[:]).then_inc(seg_t, 1)
                for q, gs in enumerate(groups):
                    if q >= 2:
                        pe.wait_ge(last_kept, q - 1)
                    for g in gs:
                        last = nc.tensor.transpose(ps_last[q % 2][:, g - gs[0], :], K.mask_r[:, g * P:(g + 1) * P], K.ident[:])
                    last.then_inc(last_t, 1)


def norm_stats(nc, dve, ch, y, ph, stats_done, var_ready, std_ready, eps, stat, mean, rstd, a, b):
    with dve.Fori(0, NT // UN) as i:
        for u in range(UN):
            nc.vector.bn_stats(stat[:, bass.ds(i * UN + u, 1), :].rearrange("p a s -> p (a s)"),
                               y[:, bass.ds(i * UN + u, 1), :].rearrange("p a s -> p (a s)")).then_inc(stats_done, 1)
    dve.wait_ge(stats_done, NT)
    ch.note(nc.vector.tensor_tensor(a[:], stat[:, :, 1], stat[:, :, 4], ALU.add))
    ch.link(nc.vector.tensor_tensor(b[:], stat[:, :, 1], stat[:, :, 4], ALU.subtract))
    ch.note(nc.vector.tensor_scalar(mean[:], a[:], 0.5, None, ALU.mult))
    ch.link(nc.vector.scalar_tensor_tensor(rstd[:], b[:], 0.25, b[:], ALU.mult, ALU.mult))
    ch.link(nc.vector.tensor_tensor(a[:], stat[:, :, 2], stat[:, :, 5], ALU.add))
    ch.link(nc.vector.scalar_tensor_tensor(b[:], a[:], 1.0 / D, rstd[:], ALU.mult, ALU.add))
    nc.vector.tensor_scalar(a[:], b[:], eps, None, ALU.add).then_inc(var_ready, 1)
    dve.wait_ge(std_ready, 1)
    ch.link(nc.vector.reciprocal(rstd[:], b[:]))
    ch.link(nc.vector.tensor_tensor(b[:], rstd[:], rstd[:], ALU.mult))
    ch.link(nc.vector.tensor_tensor(b[:], b[:], a[:], ALU.mult))
    ch.link(nc.vector.tensor_scalar(b[:], b[:], -0.5, 1.5, ALU.mult, ALU.add))
    ch.link(nc.vector.tensor_tensor(rstd[:], b[:], rstd[:], ALU.mult))


def norm_and_transpose(nc, K, name, y, xn, xnT, norm=True):
    with Phase(nc, name) as ph:
        stat = ph.sb("stat", [P, NT, 6])
        mean, rstd, a, b = (ph.sb(s, [P, NT]) for s in ("mean", "rstd", "a", "b"))
        ps = [ph.psum(f"ps{u}", [P, DC, P]) for u in range(UN)]
        stats_done, var_ready, std_ready, dv, xn_ready, turned, kept = (
            ph.sem(s) for s in ("stats_done", "var_ready", "std_ready", "dv", "xn_ready", "turned", "kept"))
        with nc.Block() as block:
            if norm:
                @block.vector
                def _(dve):
                    ch = Chain(dve, dv)
                    norm_stats(nc, dve, ch, y, ph, stats_done, var_ready, std_ready, 1e-5, stat, mean, rstd, a, b)
                    with dve.Fori(0, NT // UN) as i:
                        for u in range(UN):
                            t = i * UN + u
                            nc.vector.tensor_scalar(xn[:, bass.ds(t, 1), :].rearrange("p a s -> p (a s)"),
                                                    y[:, bass.ds(t, 1), :].rearrange("p a s -> p (a s)"),
                                                    mean[:, bass.ds(t, 1)], rstd[:, bass.ds(t, 1)],
                                                    ALU.subtract, ALU.mult).then_inc(xn_ready, 1)

            @block.tensor
            def _(pe):
                for t in range(NT):
                    if norm:
                        pe.wait_ge(xn_ready, t + 1)
                    if t >= UN:
                        pe.wait_ge(kept, t + 1 - UN)
                    for c in range(DC):
                        last = nc.tensor.transpose(ps[t % UN][:, c, :], xn[:, t, c * P:(c + 1) * P], K.ident[:])
                    last.then_inc(turned, 1)

            @block.scalar
            def _(act):
                if norm:
                    act.wait_ge(var_ready, 1)
                    nc.scalar.activation(b[:], a[:], ACT.Sqrt).then_inc(std_ready, 1)
                with act.Fori(0, NT // UN) as i:
                    for u in range(UN):
                        act.wait_ge(turned, i * UN + u + 1)
                        nc.scalar.copy(xnT[:, :, bass.ds((i * UN + u) * P, P)], ps[u][:]).then_inc(kept, 1)


class Kept:

    def __init__(self, nc, stack):
        def sb(name, shape, dt=F32):
            return stack.enter_context(nc.sbuf_tensor(name, shape, dt))

        self.x = sb("x", [P, NT, D])
        self.ident = sb("ident", [P, P])
        self.ones = sb("ones", [P, P])
        self.col = sb("col", [P, P])
        self.row = sb("row", [P, 1])
        self.izero = sb("izero", [P, BATCH], U32)
        self.rel_t = sb("rel_t", [P, STEPS])
        self.bad_t = sb("bad_t", [P, STEPS])
        self.last_t = sb("last_t", [P, STEPS])
        self.src_t = sb("src_t", [P, TAB], U32)
        self.id_t = sb("id_t", [P, TAB], U32)
        self.blk_row = sb("blk_row", [1, STEPS], I32)
        self.mask_f = sb("mask_f", [P, RUNE])
        self.mask_r = sb("mask_r", [P, RUNE])
        self.cut_f = sb("cut_f", [1, P])
        self.cut_r = sb("cut_r", [1, P])
        self.rel_rows = nc.dram_tensor("rel_rows", (STEPS, P), BF16, kind="Internal").ap()


def project(nc, K, name, xnT, w_view, att, att_heads, h_rows, a_rows, adn):
    with Phase(nc, name) as ph:
        w = ph.sb("w", [P, DC, D + 2 * HEADS])
        a_b = ph.sb("a_b", [P, 2, D])
        prod = ph.sb("prod", [P, 2, DC, D])
        red = ph.sb("red", [P, 2, DC, att_heads])
        h = ph.sb("h", [P, NT, D + 2 * HEADS])
        ps = [ph.psum(f"ps{u}", [P, D + 2 * HEADS]) for u in range(UN)]
        w_in, w_ready, dv, projected, h_kept, stored = (
            ph.sem(s) for s in ("w_in", "w_ready", "dv", "projected", "h_kept", "stored"))
        with nc.Block() as block:
            @block.sync
            def _(sp):
                n = 0
                for c in range(DC):
                    for to, frm in w_view(c):
                        sp.dma_start(to(w[:, c, :]), frm).then_inc(w_in, 16)
                        n += 1
                for a in range(2):
                    sp.dma_start(a_b[:, a, :], over_partitions(att[a])).then_inc(w_in, 16)
                assert n + 2 == w_loads(w_view)
                with sp.Fori(0, NT // UN) as i:
                    sp.wait_ge(h_kept, i * UN + UN)
                    sp.dma_start(h_rows[bass.ds(i * UN * P, UN * P), :].rearrange("(t p) d -> p t d", p=P),
                                 h[:, bass.ds(i * UN, UN), 0:D]).then_inc(stored, 16)
                sp.dma_start(a_rows.rearrange("(t p) h -> p t h", p=P), h[:, :, D:D + HEADS]).then_inc(stored, 16)
                sp.wait_ge(stored, 16 * (NT // UN + 1))

            @block.vector
            def _(dve):
                ch = Chain(dve, dv)
                ch.note(nc.vector.memset(adn[:, NT, :], 0.0))
                dve.wait_ge(w_in, 16 * w_loads(w_view))
                for a in range(2):
                    for c in range(DC):
                        ch.note(nc.vector.tensor_tensor(prod[:, a, c, :], w[:, c, 0:D], a_b[:, a, :], ALU.mult))
                ch.settle()
                for a in range(2):
                    ch.note(nc.vector.tensor_reduce(red[:, a], prod[:, a].rearrange("p c (h f) -> p c h f", h=att_heads), AX.X, ALU.add))
                ch.settle()
                for a in range(2):
                    to = w[:, :, D + a * HEADS:D + (a + 1) * HEADS]
                    frm = red[:, a] if att_heads == HEADS else red[:, a].to_broadcast([P, DC, HEADS])
                    nc.vector.tensor_copy(to, frm).then_inc(w_ready, 1)
                dve.wait_ge(h_kept, NT)
                nc.vector.tensor_copy(adn[:, 0:NT, 0:HEADS], h[:, :, D + HEADS:D + 2 * HEADS])
                if adn.shape[2] > HEADS:
                    own = adn[:, 0:NT, HEADS:2 * HEADS]
                    ch.link(nc.vector.tensor_tensor(own, h[:, :, D:D + HEADS], h[:, :, D + HEADS:D + 2 * HEADS], ALU.add))
                    nc.vector.scalar_tensor_tensor(own, own, 0.2, own, ALU.mult, ALU.max)

            @block.tensor
            def _(pe):
                pe.wait_ge(w_ready, 2)
                for t in range(NT):
                    if t >= UN:
                        pe.wait_ge(h_kept, t + 1 - UN)
                    for c in range(DC):
                        last = nc.tensor.matmul(ps[t % UN][:], xnT[:, c, t * P:(t + 1) * P], w[:, c, :], start=(c == 0), stop=(c == DC - 1))
                    last.then_inc(projected, 1)

            @block.scalar
            def _(act):
                with act.Fori(0, NT // UN) as i:
                    for u in range(UN):
                        act.wait_ge(projected, i * UN + u + 1)
                        nc.scalar.copy(h[:, bass.ds(i * UN + u, 1), :].rearrange("p a d -> p (a d)"), ps[u][:]).then_inc(h_kept, 1)


def w_loads(w_view):
    return sum(len(w_view(c)) for c in range(DC)) + 2


def gather_batches(nc, pool, K, idx, table, stage, idx_slot, copied, copied_seen, gathered, free):
    with pool.Fori(0, NB // SLOTS) as j:
        for m in range(SLOTS):
            n = j * SLOTS + m
            pool.wait_ge(free, n + 1)
            nc.gpsimd.tensor_tensor(idx_slot[:, m, :], idx[:, bass.ds(n * BATCH, BATCH)], K.izero[:], ALU.add).then_inc(copied, 1)
            pool.wait_ge(copied, n + 1)
            pool.sem_inc(copied_seen, 1)
            for u in range(BATCH):
                nc.gpsimd.indirect_dma_start(out=stage[:, m, u, :], out_offset=None, in_=table,
                                             in_offset=bass.IndirectOffsetOnAxis(ap=idx_slot[:, m, u:u + 1], axis=0)).then_inc(gathered[m], 16)


def edge_logits(nc, K, name, a_rows, adn, L, S=None):
    AW = HEADS if S is None else 2 * HEADS
    with Phase(nc, name) as ph:
        stage = ph.sb("stage", [P, SLOTS, BATCH, HEADS])
        idx_slot = ph.sb("idx_slot", [P, SLOTS, BATCH], U32)
        rel_b = ph.sb("rel_b", [P, SLOTS, BATCH * P], BF16)
        hot = ph.sb("hot", [P, 2, BATCH * P])
        t1 = ph.sb("t1", [P, 2, BATCH, HEADS])
        t2 = ph.sb("t2", [P, 2, BATCH, HEADS])
        ps = [ph.psum(f"ps{m}", [P, BATCH, AW]) for m in range(2)]
        copied, copied_seen, free, hot_built, added, z_done, L_done = (ph.sem(s) for s in ("copied", "copied_seen", "free", "hot_built", "added", "z_done", "L_done"))
        gathered = [ph.sem(f"gathered{m}") for m in range(SLOTS)]
        rel_in = [ph.sem(f"rel_in{m}") for m in range(SLOTS)]
        biased = ph.sem("biased")
        with nc.Block() as block:
            @block.gpsimd
            def _(pool):
                gather_batches(nc, pool, K, K.src_t, a_rows, stage, idx_slot, copied, copied_seen, gathered, free)

            @block.sync
            def _(sp):
                with sp.Fori(0, NB // SLOTS) as j:
                    for m in range(SLOTS):
                        n = j * SLOTS + m
                        sp.wait_ge(hot_built, n + 1)
                        sp.dma_start(rel_b[:, m, :], over_partitions(K.rel_rows[bass.ds(n * BATCH, BATCH), :].rearrange("s e -> (s e)"))).then_inc(rel_in[m], 16)

            @block.vector
            def _(dve):
                dve.sem_inc(hot_built, SLOTS)
                dve.sem_inc(free, SLOTS)
                dve.sem_inc(z_done, 2)

                def build(n, j, m):
                    dve.wait_ge(rel_in[m], j * 16 + 16)
                    dve.wait_ge(added, n * BATCH + BATCH)
                    nc.vector.tensor_scalar(hot[:, m % 2, :], rel_b[:, m, :], K.row[:], None, ALU.is_equal).then_inc(hot_built, 1)

                def finish(n, j, m):
                    dve.wait_ge(gathered[m], j * (16 * BATCH) + 16 * BATCH)
                    b = bass.ds(n * BATCH, BATCH)
                    nc.vector.tensor_tensor(t1[:, m % 2], stage[:, m], bcast(K.bad_t[:, b], HEADS), ALU.add).then_inc(free, 1)
                    dve.wait_ge(free, n + 1 + SLOTS)
                    dve.wait_ge(added, n * BATCH + 3 * BATCH)
                    if S is not None:
                        nc.vector.tensor_tensor(S[:, b, :], ps[m % 2][:, :, HEADS:AW], bcast(K.bad_t[:, b], HEADS), ALU.add)
                    nc.vector.tensor_tensor(t2[:, m % 2], t1[:, m % 2], ps[m % 2][:, :, 0:HEADS], ALU.add).then_inc(z_done, 1)
                    dve.wait_ge(z_done, n + 3)
                    nc.vector.scalar_tensor_tensor(L[:, b, :], t2[:, m % 2], 0.2, t2[:, m % 2], ALU.mult, ALU.max).then_inc(L_done, 1)

                build(0, 0, 0)
                with dve.Fori(0, NB // SLOTS - 1) as j:
                    for m in range(SLOTS):
                        build(j * SLOTS + m + 1, j if m < SLOTS - 1 else j + 1, (m + 1) % SLOTS)
                        finish(j * SLOTS + m, j, m)
                j = NB // SLOTS - 1
                for m in range(SLOTS):
                    if m < SLOTS - 1:
                        build(j * SLOTS + m + 1, j, m + 1)
                    finish(j * SLOTS + m, j, m)

            @block.tensor
            def _(pe):
                pe.sem_inc(added, 2 * BATCH)
                with pe.Fori(0, NB // SLOTS) as j:
                    for m in range(SLOTS):
                        n = j * SLOTS + m
                        pe.wait_ge(hot_built, n + 1 + SLOTS)
                        pe.wait_ge(z_done, n + 1)
                        blks = [pe.value_load(K.blk_row[0:1, bass.ds(n * BATCH + u, 1)], min_val=0, max_val=NT) for u in range(BATCH)]
                        for u, blk in enumerate(blks):
                            nc.tensor.matmul(ps[m % 2][:, u, :], hot[:, m % 2, u * P:(u + 1) * P],
                                             adn[:, bass.ds(blk, 1), :].rearrange("p a h -> p (a h)"), start=True, stop=True).then_inc(added, 1)


def segment_softmax(nc, K, name, L, S=None):
    with Phase(nc, name) as ph:
        lt = ph.sb("lt", [P, RUNE])
        ft = ph.sb("ft", [P, RUNE])
        last_row = ph.sb("last_row", [1, 2, P])
        carry = ph.sb("carry", [1, 2, P + 2])
        carry_kh = ph.sb("carry_kh", [1, 2, P])
        init = ph.sb("init", [P, 2])
        PAIR = 4
        ps = [ph.psum(f"ps{u}", [P, PAIR, P]) for u in range(2)]
        ps_row = ph.psum("ps_row", [P, 2, P])
        ps_init = ph.psum("ps_init", [P, 2])
        packed = ph.sem("packed")
        turned, lt_kept, dv, col_ready, row_ready, carry_ready, init_ready, maxed, turned2, L_less, ex = (
            ph.sem(s) for s in ("turned", "lt_kept", "dv", "col_ready", "row_ready", "carry_ready", "init_ready", "maxed", "turned2", "L_less", "ex"))
        groups = [range(g, min(g + PAIR, RUN)) for g in range(0, RUN, PAIR)]
        by_run = L[:].rearrange("p (k g) h -> p g k h", g=RUN)
        s_by_run = None if S is None else S[:].rearrange("p (k g) h -> p g k h", g=RUN)
        with nc.Block() as block:
            @block.tensor
            def _(pe):
                for q, gs in enumerate(groups):
                    pe.wait_ge(packed, q + 1)
                    if q >= 2:
                        pe.wait_ge(lt_kept, q - 1)
                    for g in gs:
                        last = nc.tensor.transpose(ps[q % 2][:, g - gs[0], :], ft[:, g * P:(g + 1) * P], K.ident[:])
                    last.then_inc(turned, 1)
                for d in range(2):
                    pe.wait_ge(col_ready, d + 1)
                    col = ft[:, RUNE - 1:RUNE] if d == 0 else lt[:, 0:1]
                    nc.tensor.transpose(ps_row[0:1, d, :], col, K.ident[:]).then_inc(row_ready, 1)
                    pe.wait_ge(carry_ready, d + 1)
                    nc.tensor.transpose(ps_init[:, d:d + 1], carry_kh[:, d, :], K.ident[0:1, 0:1]).then_inc(init_ready, 1)
                pe.wait_ge(maxed, 1)
                for q, gs in enumerate(groups):
                    if q >= 2:
                        pe.wait_ge(L_less, q - 1)
                    for g in gs:
                        last = nc.tensor.transpose(ps[q % 2][:, g - gs[0], :], lt[:, g * P:(g + 1) * P], K.ident[:])
                    last.then_inc(turned2, 1)

            if S is None:
                @block.gpsimd
                def _(pool):
                    for q, gs in enumerate(groups):
                        nc.gpsimd.tensor_copy(ft[:, gs[0] * P:(gs[-1] + 1) * P].rearrange("p (g k h) -> p g k h", k=KK, h=HEADS),
                                              by_run[:, gs[0]:gs[-1] + 1]).then_inc(packed, 1)

            @block.scalar
            def _(act):
                for q, gs in enumerate(groups):
                    act.wait_ge(turned, q + 1)
                    nc.scalar.copy(lt[:, gs[0] * P:(gs[-1] + 1) * P].rearrange("p (g e) -> p g e", e=P), ps[q % 2][:, 0:len(gs), :]).then_inc(lt_kept, 1)
                act.wait_ge(L_less, len(groups))
                if S is not None:
                    nc.scalar.activation(S[:], S[:], ACT.Exp).then_inc(ex, 1)
                nc.scalar.activation(L[:], L[:], ACT.Exp)

            @block.vector
            def _(dve):
                ch = Chain(dve, dv)
                ch.link(nc.vector.memset(carry[:], NEG))
                if S is not None:
                    for gs in groups:
                        for g in gs:
                            ins = nc.vector.tensor_tensor(ft[:, g * P:(g + 1) * P].rearrange("p (k h) -> p k h", h=HEADS),
                                                          by_run[:, g], s_by_run[:, g], ALU.max)
                        ins.then_inc(packed, 1)
                dve.wait_ge(lt_kept, len(groups))
                for d in range(2):
                    frm, to, mask = (lt, ft, K.mask_f) if d == 0 else (ft, lt, K.mask_r)
                    way = slice(None, None, 1) if d == 0 else slice(None, None, -1)
                    ch.link(nc.vector.tensor_tensor_scan(to[:, way], mask[:, way], frm[:, way], NEG, ALU.add, ALU.max))
                    dve.sem_inc(col_ready, 1)
                    dve.wait_ge(row_ready, d + 1)
                    ch.link(nc.vector.tensor_copy(last_row[:, d, :].rearrange("o (h k) -> o h k", h=HEADS),
                                                  ps_row[0:1, d, :].rearrange("o (k h) -> o h k", h=HEADS)))
                    cut = (K.cut_f, K.cut_r)[d]
                    ch.link(nc.vector.tensor_tensor_scan(carry[:, d, 1:P + 1][:, way], cut[:, way], last_row[:, d, :][:, way], NEG, ALU.add, ALU.max))
                    shifted = (carry[:, 0, 0:P] if d == 0 else carry[:, 1, 2:P + 2]).rearrange("o (h k) -> o h k", h=HEADS)
                    edge = 0 if d == 0 else KK - 1
                    ch.link(nc.vector.tensor_copy(carry_kh[:, d, :].rearrange("o (k h) -> o h k", h=HEADS), shifted))
                    ch.link(nc.vector.memset(carry_kh[:, d, edge * HEADS:(edge + 1) * HEADS], NEG))
                    dve.sem_inc(carry_ready, 1)
                    dve.wait_ge(init_ready, d + 1)
                    ch.link(nc.vector.tensor_copy(init[:, d:d + 1], ps_init[:, d:d + 1]))
                    ch.link(nc.vector.tensor_tensor_scan(to[:, way], mask[:, way], frm[:, way], init[:, d:d + 1], ALU.add, ALU.max))
                dve.sem_inc(maxed, 1)
                for q, gs in enumerate(groups):
                    dve.wait_ge(turned2, q + 1)
                    part = by_run[:, gs[0]:gs[-1] + 1]
                    for g in gs:
                        ins = nc.vector.tensor_tensor(by_run[:, g], by_run[:, g],
                                                      ps[q % 2][:, g - gs[0], :].rearrange("p (k h) -> p k h", h=HEADS), ALU.subtract)
                        if S is not None:
                            ins = nc.vector.tensor_tensor(s_by_run[:, g], s_by_run[:, g],
                                                          ps[q % 2][:, g - gs[0], :].rearrange("p (k h) -> p k h", h=HEADS), ALU.subtract)
                    ins.then_inc(L_less, 1)
                if S is not None:
                    dve.wait_ge(ex, 1)
                    nc.vector.tensor_tensor(S[:], S[:], bcast(K.last_t[:], HEADS), ALU.mult)


def aggregate(nc, K, name, L, accs, h_rows, edge_rows=None, S=None):
    ROW = D + HEADS * (1 if S is None else 2)
    with Phase(nc, name) as ph:
        stage = ph.sb("stage", [P, SLOTS, BATCH, D])
        idx_slot = ph.sb("idx_slot", [P, SLOTS, BATCH], U32)
        hot = ph.sb("hot", [P, 2, BATCH, P])
        msg = ph.sb("msg", [P, 2, BATCH, ROW])
        PSL = 8
        claimed = ph.sem("claimed")
        per_slot = 16 * BATCH if edge_rows is None else 16
        ps = [ph.psum(f"ps{m}", [P, ROW]) for m in range(PSL)]
        copied, copied_seen, free, hot_built, msg_built, w_placed, summed, added = (
            ph.sem(s) for s in ("copied", "copied_seen", "free", "hot_built", "msg_built", "w_placed", "summed", "added"))
        gathered = [ph.sem(f"gathered{m}") for m in range(SLOTS)]
        with nc.Block() as block:
            if edge_rows is None:
                @block.gpsimd
                def _(pool):
                    gather_batches(nc, pool, K, K.src_t, h_rows, stage, idx_slot, copied, copied_seen, gathered, free)
            else:
                @block.sync
                def _(sp):
                    with sp.Fori(0, NB // SLOTS) as j:
                        for m in range(SLOTS):
                            n = j * SLOTS + m
                            sp.wait_ge(free, n + 1)
                            sp.sem_inc(claimed, 1)
                            sp.dma_start(stage[:, m], edge_rows[bass.ds(n * BATCH, BATCH)].rearrange("s p d -> p s d")).then_inc(gathered[m], 16)

            @block.vector
            def _(dve):
                dve.sem_inc(free, SLOTS)
                nc.vector.memset(accs[0], 0.0)
                nc.vector.memset(accs[1], 0.0).then_inc(added, PSL)

                def build(n, j, m):
                    b = bass.ds(n * BATCH, BATCH)
                    dve.wait_ge(summed, n * BATCH + BATCH)
                    nc.vector.tensor_tensor(hot[:, m % 2], K.col[:].unsqueeze(1).to_broadcast([P, BATCH, P]),
                                            bcast(K.rel_t[:, b], P), ALU.is_equal).then_inc(hot_built, 1)
                    dve.wait_ge(gathered[m], j * per_slot + per_slot)
                    nc.vector.tensor_tensor(msg[:, m % 2, :, 0:D].rearrange("p s (h c) -> p s h c", h=HEADS),
                                            stage[:, m].rearrange("p s (h c) -> p s h c", h=HEADS),
                                            bcast(L[:, b, :], C), ALU.mult).then_inc(free, 1)

                def add(n, j, m):
                    blks = [dve.value_load(K.blk_row[0:1, bass.ds(n * BATCH + u, 1)], min_val=0, max_val=NT) for u in range(BATCH)]
                    for u, blk in enumerate(blks):
                        q = n * BATCH + u
                        dve.wait_ge(summed, q + 1 + 2 * BATCH)
                        dve.wait_ge(added, q + PSL - 1)
                        to = accs[u % 2][:, bass.ds(blk, 1), :].rearrange("p a d -> p (a d)")
                        nc.vector.tensor_tensor(to, to, ps[u][:], ALU.add).then_inc(added, 1)

                build(0, 0, 0)
                with dve.Fori(0, NB // SLOTS - 1) as j:
                    for m in range(SLOTS):
                        build(j * SLOTS + m + 1, j if m < SLOTS - 1 else j + 1, (m + 1) % SLOTS)
                        add(j * SLOTS + m, j, m)
                j = NB // SLOTS - 1
                for m in range(SLOTS):
                    if m < SLOTS - 1:
                        build(j * SLOTS + m + 1, j, m + 1)
                    add(j * SLOTS + m, j, m)

            @block.scalar
            def _(act):
                with act.Fori(0, NB // SLOTS) as j:
                    for m in range(SLOTS):
                        n = j * SLOTS + m
                        act.wait_ge(summed, n * BATCH + BATCH)
                        if S is not None:
                            nc.scalar.copy(msg[:, m % 2, :, D + HEADS:ROW], S[:, bass.ds(n * BATCH, BATCH), :])
                        nc.scalar.copy(msg[:, m % 2, :, D:D + HEADS], L[:, bass.ds(n * BATCH, BATCH), :]).then_inc(w_placed, 1)

            @block.tensor
            def _(pe):
                pe.sem_inc(summed, 2 * BATCH)
                with pe.Fori(0, NB // SLOTS) as j:
                    for m in range(SLOTS):
                        n = j * SLOTS + m
                        pe.wait_ge(hot_built, n + 1)
                        pe.wait_ge(free, n + 1 + SLOTS)
                        pe.wait_ge(w_placed, n + 1)
                        for u in range(BATCH):
                            pe.wait_ge(added, n * BATCH + u + 1)
                            nc.tensor.matmul(ps[u][:], hot[:, m % 2, u, :], msg[:, m % 2, u, :], start=True, stop=True).then_inc(summed, 1)


def finish_gat(nc, K, name, accs, eps, bias, out, relu=False, add=True, own_rows=None):
    acc = accs[0]
    with Phase(nc, name) as ph:
        r = ph.sb("r", [P, NT, HEADS])
        b = ph.sb("b", [P, D])
        own = None if own_rows is None else ph.sb("own", [P, NT, D])
        dv, bias_in, own_in = ph.sem("dv"), ph.sem("bias_in"), ph.sem("own_in")
        with nc.Block() as block:
            if bias is not None:
                @block.sync
                def _(sp):
                    sp.dma_start(b[:], over_partitions(bias)).then_inc(bias_in, 16)
                    if own is not None:
                        sp.dma_start(own[:], own_rows.rearrange("(t p) d -> p t d", p=P)).then_inc(own_in, 16)

            @block.vector
            def _(dve):
                ch = Chain(dve, dv)
                ch.link(nc.vector.tensor_tensor(acc[:, 0:NT, :], acc[:, 0:NT, :], accs[1][:, 0:NT, :], ALU.add))
                if own_rows is not None:
                    w = acc[:, 0:NT, D + HEADS:D + 2 * HEADS]
                    den = acc[:, 0:NT, D:D + HEADS]
                    ch.link(nc.vector.tensor_tensor(r[:], den, w, ALU.add))
                    ch.link(nc.vector.tensor_scalar(r[:], r[:], 0.0, None, ALU.is_equal))
                    ch.link(nc.vector.tensor_tensor(w, w, r[:], ALU.add))
                    ch.link(nc.vector.tensor_tensor(den, den, w, ALU.add))
                    dve.wait_ge(own_in, 16)
                    for h in range(HEADS):
                        part = own[:, :, h * C:(h + 1) * C]
                        ch.note(nc.vector.tensor_tensor(part, part, bcast(w[:, :, h], C), ALU.mult))
                    ch.settle()
                    ch.link(nc.vector.tensor_tensor(acc[:, 0:NT, 0:D], acc[:, 0:NT, 0:D], own[:], ALU.add))
                ch.link(nc.vector.tensor_scalar(r[:], acc[:, 0:NT, D:D + HEADS], eps, None, ALU.add))
                ch.link(nc.vector.reciprocal(r[:], r[:]))
                body = acc[:, 0:NT, 0:D]
                for h in range(HEADS):
                    part = acc[:, 0:NT, h * C:(h + 1) * C]
                    ch.note(nc.vector.tensor_tensor(part, part, bcast(r[:, :, h], C), ALU.mult))
                ch.settle()
                if bias is not None:
                    dve.wait_ge(bias_in, 16)
                    ch.link(nc.vector.tensor_tensor(body, body, b[:].unsqueeze(1).to_broadcast([P, NT, D]), ALU.add))
                if relu:
                    ch.link(nc.vector.scalar_tensor_tensor(out[:], body, 0.0, out[:], ALU.max, ALU.add))
                elif add:
                    ch.link(nc.vector.tensor_tensor(out[:], out[:], body, ALU.add))
                else:
                    ch.link(nc.vector.tensor_copy(out[:], body))


def gat_layer(nc, K, name, w_view, att, att_heads, eps, bias, src_x=None, dst_x=None, relu=False, add=True, norm=True, loops=False, odd=None):
    AW = 2 * HEADS if loops else HEADS
    h_rows = nc.dram_tensor(f"{name}_h_rows", (NPAD, D), F32, kind="Internal").ap()
    a_rows = nc.dram_tensor(f"{name}_a_rows", (NPAD, HEADS), F32, kind="Internal").ap()
    src_x = K.x if src_x is None else src_x
    dst_x = K.x if dst_x is None else dst_x
    with Phase(nc, name + "_attn") as keep:
        adn = keep.sb("adn", [P, NT + 1, AW])
        L = keep.sb("L", [P, STEPS, HEADS])
        S = keep.sb("S", [P, STEPS, HEADS]) if loops else None
        with Phase(nc, name + "_nodes") as nodes:
            xnT = nodes.sb("xnT", [P, DC, NPAD])
            xn = nodes.sb("xn", [P, NT, D]) if norm else src_x
            norm_and_transpose(nc, K, name + "_norm", src_x, xn, xnT, norm)
            project(nc, K, name + "_proj", xnT, w_view, att, att_heads, h_rows, a_rows, adn)
        edge_logits(nc, K, name + "_logit", a_rows, adn, L, S)
        segment_softmax(nc, K, name + "_soft", L, S)
        if odd is None:
            odd = keep.sb("odd", [P, NT + 1, D + AW])[:]
        accs = [keep.sb("acc", [P, NT + 1, D + AW])[:], odd]
        aggregate(nc, K, name + "_agg", L, accs, h_rows, None, S)
        finish_gat(nc, K, name + "_fin", accs, eps, bias, dst_x, relu, add, h_rows if loops else None)


GT = 5
GN = GT * P
HALF = GN // 2
NG = NT // GT
Y0 = 2 * NG * GT


def router_logits(nc, K, name, xnT, wr, br, E, lg):
    with Phase(nc, name) as ph:
        w = ph.sb("w", [P, DC, E])
        b = ph.sb("b", [P, E])
        ps = ph.psum("ps", [P, NT, E])
        w_in, made = ph.sem("w_in"), ph.sem("made")
        with nc.Block() as block:
            @block.sync
            def _(sp):
                sp.dma_start(w[:], wr.rearrange("(c p) e -> p c e", p=P)).then_inc(w_in, 16)
                sp.dma_start(b[:], over_partitions(br)).then_inc(w_in, 16)

            @block.tensor
            def _(pe):
                pe.wait_ge(w_in, 32)
                for t in range(NT):
                    for c in range(DC):
                        last = nc.tensor.matmul(ps[:, t, :], xnT[:, c, t * P:(t + 1) * P], w[:, c, :], start=(c == 0), stop=(c == DC - 1))
                last.then_inc(made, 1)

            @block.vector
            def _(dve):
                dve.wait_ge(w_in, 32)
                dve.wait_ge(made, 1)
                nc.vector.tensor_tensor(lg[:], ps[:], b[:].unsqueeze(1).to_broadcast([P, NT, E]), ALU.add)


def top2_gates(nc, K, name, lg, E, gates):
    with Phase(nc, name) as ph:
        m8 = ph.sb("m8", [P, NT, 8])
        i8 = ph.sb("i8", [P, NT, 8], U32)
        best = ph.sb("best", [P, 2, NT])
        gap = ph.sb("gap", [P, NT])
        w = ph.sb("w", [P, 2, NT])
        hot = ph.sb("hot", [P, NT, E])
        dv, gap_ready, exp_ready = ph.sem("dv"), ph.sem("gap_ready"), ph.sem("exp_ready")
        with nc.Block() as block:
            @block.vector
            def _(dve):
                ch = Chain(dve, dv)
                for t in range(NT):
                    ch.note(nc.vector.max(m8[:, t, :], lg[:, t, :]))
                ch.settle()
                for t in range(NT):
                    ch.note(nc.vector.max_index(i8[:, t, :], m8[:, t, :], lg[:, t, :]))
                nc.vector.tensor_tensor(gap[:], m8[:, :, 1], m8[:, :, 0], ALU.subtract).then_inc(gap_ready, 1)
                ch.settle()
                for a in range(2):
                    ch.note(nc.vector.tensor_copy(best[:, a, :], i8[:, :, a]))
                dve.wait_ge(exp_ready, 1)
                ch.link(nc.vector.tensor_scalar(w[:, 0, :], gap[:], 1.0, None, ALU.add))
                ch.link(nc.vector.reciprocal(w[:, 0, :], w[:, 0, :]))
                ch.link(nc.vector.tensor_tensor(w[:, 1, :], gap[:], w[:, 0, :], ALU.mult))
                for a, to in ((0, gates), (1, hot)):
                    ch.link(nc.vector.tensor_tensor(to[:], K.col[:, 0:E].unsqueeze(1).to_broadcast([P, NT, E]), bcast(best[:, a, :], E), ALU.is_equal))
                    ch.link(nc.vector.tensor_tensor(to[:], to[:], bcast(w[:, a, :], E), ALU.mult))
                nc.vector.tensor_tensor(gates[:], gates[:], hot[:], ALU.add)

            @block.scalar
            def _(act):
                act.wait_ge(gap_ready, 1)
                nc.scalar.activation(gap[:], gap[:], ACT.Exp).then_inc(exp_ready, 1)


def softmax_gates(nc, K, name, lg, E, gates):
    with Phase(nc, name) as ph:
        m = ph.sb("m", [P, NT])
        dv, less, ex = ph.sem("dv"), ph.sem("less"), ph.sem("ex")
        with nc.Block() as block:
            @block.vector
            def _(dve):
                ch = Chain(dve, dv)
                ch.link(nc.vector.tensor_reduce(m[:], lg[:], AX.X, ALU.max))
                nc.vector.tensor_tensor(lg[:], lg[:], bcast(m[:], E), ALU.subtract).then_inc(less, 1)
                dve.wait_ge(ex, 1)
                ch.link(nc.vector.tensor_reduce(m[:], lg[:], AX.X, ALU.add))
                ch.link(nc.vector.reciprocal(m[:], m[:]))
                nc.vector.tensor_tensor(gates[:], lg[:], bcast(m[:], E), ALU.mult)

            @block.scalar
            def _(act):
                act.wait_ge(less, 1)
                nc.scalar.activation(lg[:], lg[:], ACT.Exp).then_inc(ex, 1)


def global_gates(nc, K, name, xnT, wr, br, capacity, gates, picked_w, picked):
    E = 8
    with Phase(nc, name) as ph:
        w = ph.sb("w", [P, DC, E])
        b = ph.sb("b", [1, E])
        feat = ph.sb("feat", [P, DC])
        r = [ph.sb(f"r{n}", [1, E]) for n in range(3)]
        s = ph.sb("s", [1, 4])
        m8 = ph.sb("m8", [1, 8])
        i8 = ph.sb("i8", [1, 8], U32)
        best = ph.sb("best", [1, 2])
        row = ph.sb("row", [1, E + 2])
        ps = ph.psum("ps", [P, 64])
        w_in, dv, feat_ready, made, to_exp, ex, row_ready, spread = (
            ph.sem(n) for n in ("w_in", "dv", "feat_ready", "made", "to_exp", "ex", "row_ready", "spread"))
        with nc.Block() as block:
            @block.sync
            def _(sp):
                sp.dma_start(w[:], wr.rearrange("(c p) e -> p c e", p=P)).then_inc(w_in, 16)
                sp.dma_start(b[:], br.rearrange("(a e) -> a e", a=1)).then_inc(w_in, 16)

            @block.tensor
            def _(pe):
                pe.wait_ge(w_in, 32)
                pe.wait_ge(feat_ready, 1)
                for c in range(DC):
                    last = nc.tensor.matmul(ps[0:1, 0:E], feat[:, c:c + 1], w[:, c, :], start=(c == 0), stop=(c == DC - 1))
                last.then_inc(made, 1)
                pe.wait_ge(row_ready, 1)
                nc.tensor.matmul(ps[:, 32:32 + E + 2], K.ones[0:1, :], row[:], start=True, stop=True).then_inc(spread, 1)

            @block.vector
            def _(dve):
                ch = Chain(dve, dv)
                ch.link(nc.vector.tensor_reduce(feat[:], xnT[:], AX.X, ALU.add))
                nc.vector.tensor_scalar(feat[:], feat[:], 1.0 / N_NODES, None, ALU.mult).then_inc(feat_ready, 1)
                dve.wait_ge(w_in, 32)
                dve.wait_ge(made, 1)
                ch.link(nc.vector.tensor_tensor(r[0][:], ps[0:1, 0:E], b[:], ALU.add))

                def softmax(n):
                    ch.link(nc.vector.tensor_reduce(s[:, 0:1], r[0][:], AX.X, ALU.max))
                    nc.vector.tensor_scalar(r[1][:], r[0][:], s[:, 0:1], None, ALU.subtract).then_inc(to_exp, 1)
                    dve.wait_ge(ex, n)
                    ch.link(nc.vector.tensor_reduce(s[:, 1:2], r[1][:], AX.X, ALU.add))
                    ch.link(nc.vector.reciprocal(s[:, 2:3], s[:, 1:2]))
                    ch.link(nc.vector.tensor_scalar(r[0][:], r[1][:], s[:, 2:3], None, ALU.mult))

                softmax(1)
                ch.link(nc.vector.tensor_scalar(r[2][:], r[0][:], float(N_NODES), capacity, ALU.mult, ALU.max))
                ch.link(nc.vector.reciprocal(r[1][:], r[2][:]))
                ch.link(nc.vector.tensor_scalar(r[2][:], r[1][:], capacity, None, ALU.mult))
                ch.link(nc.vector.tensor_tensor(r[0][:], r[0][:], r[2][:], ALU.mult))
                softmax(2)
                ch.link(nc.vector.max(m8[:], r[0][:]))
                ch.link(nc.vector.max_index(i8[:], m8[:], r[0][:]))
                ch.note(nc.vector.tensor_copy(best[:], i8[:, 0:2]))
                ch.note(nc.vector.tensor_copy(picked[:], i8[:, 0:2]))
                nc.vector.tensor_tensor(r[1][:, 0:1], m8[:, 1:2], m8[:, 0:1], ALU.subtract).then_inc(to_exp, 1)
                dve.wait_ge(ex, 3)
                ch.link(nc.vector.tensor_scalar(s[:, 0:1], r[1][:, 0:1], 1.0, None, ALU.add))
                ch.link(nc.vector.reciprocal(row[:, E:E + 1], s[:, 0:1]))
                ch.link(nc.vector.tensor_tensor(row[:, E + 1:E + 2], row[:, E:E + 1], r[1][:, 0:1], ALU.mult))
                ch.link(nc.vector.tensor_scalar(r[0][:], K.col[0:1, 0:E], best[:, 0:1], row[:, E:E + 1], ALU.is_equal, ALU.mult))
                ch.link(nc.vector.tensor_scalar(r[2][:], K.col[0:1, 0:E], best[:, 1:2], row[:, E + 1:E + 2], ALU.is_equal, ALU.mult))
                nc.vector.tensor_tensor(row[:, 0:E], r[0][:], r[2][:], ALU.add).then_inc(row_ready, 1)
                dve.wait_ge(spread, 1)
                nc.vector.tensor_copy(gates[:], ps[:, 32:32 + E].unsqueeze(1).to_broadcast([P, NT, E]))
                nc.vector.tensor_copy(picked_w[:], ps[:, 32 + E:32 + E + 2].unsqueeze(1).to_broadcast([P, NT, 2]))

            @block.scalar
            def _(act):
                for n in range(3):
                    act.wait_ge(to_exp, n + 1)
                    part = r[1][:] if n < 2 else r[1][:, 0:1]
                    nc.scalar.activation(part, part, ACT.Exp).then_inc(ex, 1)


def gated_bias(nc, K, name, gates, E, b2, acc, residual):
    with Phase(nc, name) as ph:
        gT = ph.sb("gT", [E, NT, P])
        b = ph.sb("b", [E, D])
        ps = [ph.psum(f"ps{m}", [P, D]) for m in range(4)]
        psg = [ph.psum(f"psg{m}", [E, P]) for m in range(4)]
        b_in, turned, kept, made, added = (ph.sem(n) for n in ("b_in", "turned", "kept", "made", "added"))
        with nc.Block() as block:
            @block.sync
            def _(sp):
                sp.dma_start(b[:], b2).then_inc(b_in, 16)

            @block.tensor
            def _(pe):
                pe.wait_ge(b_in, 16)
                for t in range(NT + 1):
                    if t < NT:
                        if t >= 4:
                            pe.wait_ge(kept, t - 3)
                        nc.tensor.transpose(psg[t % 4][:], gates[:, t, :], K.ident[:]).then_inc(turned, 1)
                    if t >= 1:
                        pe.wait_ge(kept, t)
                        if t >= 5:
                            pe.wait_ge(added, t - 4)
                        nc.tensor.matmul(ps[(t - 1) % 4][:], gT[:, t - 1, :], b[:], start=True, stop=True).then_inc(made, 1)

            @block.scalar
            def _(act):
                for t in range(NT):
                    act.wait_ge(turned, t + 1)
                    nc.scalar.copy(gT[:, t, :], psg[t % 4][:]).then_inc(kept, 1)

            @block.vector
            def _(dve):
                for t in range(NT):
                    dve.wait_ge(made, t + 1)
                    if residual:
                        nc.vector.tensor_tensor(acc[:, t, :], acc[:, t, :], ps[t % 4][:], ALU.add).then_inc(added, 1)
                    else:
                        nc.vector.tensor_copy(acc[:, t, :], ps[t % 4][:]).then_inc(added, 1)


def experts(nc, K, name, xnT, acc, gates, E, w1, b1, w2, func, F, picked=None):
    FC = F // P
    NA = 4
    tiles_a = 2 * FC
    assert tiles_a % NA == 0 and E % 2 == 0
    PAIRS = E // 2
    PER = 2 * NG
    with Phase(nc, name) as ph:
        w1_s = ph.sb("w1", [P, 2, DC, F])
        w2_s = ph.sb("w2", [P, 2, FC, D])
        b1_s = ph.sb("b1", [P, 2, FC])
        hT = ph.sb("hT", [P, 2, FC, GN])
        psa = [ph.psum(f"psa{m}", [P, HALF]) for m in range(NA)]
        psb = [ph.psum(f"psb{m}", [P, D]) for m in range(2)]
        w_in = [ph.sem(f"w_in{m}") for m in range(2)]
        claimed, h_made, h_kept, y_done, added = (ph.sem(n) for n in ("claimed", "h_made", "h_kept", "y_done", "added"))

        def pairs(eng, body):
            if PAIRS > 1:
                with eng.Fori(0, PAIRS - 1) as j:
                    body(j, False)
            body(PAIRS - 1, True)

        with nc.Block() as block:
            @block.sync
            def _(sp):
                def load(j, last):
                    for a in range(2):
                        e = j * 2 + a
                        sp.wait_ge(y_done, e * (NG * GT) + (Y0 - NG * GT))
                        sp.sem_inc(claimed, 1)
                        if picked is not None:
                            e = sp.value_load(picked[0:1, a:a + 1], min_val=0, max_val=w1.shape[0] - 1)
                        sp.dma_start(b1_s[:, a:a + 1, :], b1[bass.ds(e, 1)].rearrange("e (c p) -> p e c", p=P)).then_inc(w_in[a], 16)
                        sp.dma_start(w1_s[:, a], w1[bass.ds(e, 1)].rearrange("a (c p) f -> p (a c) f", p=P)).then_inc(w_in[a], 16)
                        sp.dma_start(w2_s[:, a], w2[bass.ds(e, 1)].rearrange("a (c p) d -> p (a c) d", p=P)).then_inc(w_in[a], 16)

                pairs(sp, load)

            @block.tensor
            def _(pe):
                pe.sem_inc(y_done, Y0)

                def hidden(u, v, j):
                    a, g = v // NG, v % NG
                    if g == 0:
                        pe.wait_ge(w_in[a], j * 48 + 48)
                    for n in range(tiles_a):
                        f, half = n // 2, n % 2
                        pe.wait_ge(h_kept, u * tiles_a + n + 1)
                        for c in range(DC):
                            at = g * GN + half * HALF
                            last = nc.tensor.matmul(psa[n % NA][:], w1_s[:, a, c, f * P:(f + 1) * P], xnT[:, c, at:at + HALF],
                                                    start=(c == 0), stop=(c == DC - 1))
                        last.then_inc(h_made, 1)

                def output(u, v):
                    a, g = v // NG, v % NG
                    pe.wait_ge(h_kept, u * tiles_a + tiles_a + NA)
                    for t in range(GT):
                        pe.wait_ge(added, u * GT + t + 1)
                        for f in range(FC):
                            last = nc.tensor.matmul(psb[(v * GT + t) % 2][:], hT[:, v % 2, f, t * P:(t + 1) * P], w2_s[:, a, f, :],
                                                    start=(f == 0), stop=(f == FC - 1))
                        last.then_inc(y_done, 1)

                hidden(0, 0, 0)

                def pair(j, last):
                    for v in range(PER):
                        if v < PER - 1:
                            hidden(j * PER + v + 1, v + 1, j)
                        elif not last:
                            hidden(j * PER + v + 1, 0, j + 1)
                        output(j * PER + v, v)

                pairs(pe, pair)

            @block.scalar
            def _(act):
                act.sem_inc(h_kept, NA)

                def pair(j, last):
                    for v in range(PER):
                        u = j * PER + v
                        if v % NG == 0:
                            act.wait_ge(w_in[v // NG], j * 48 + 48)
                        act.wait_ge(y_done, u * GT + (Y0 - GT))
                        for n in range(tiles_a):
                            f, half = n // 2, n % 2
                            act.wait_ge(h_made, u * tiles_a + n + 1)
                            nc.scalar.activation(hT[:, v % 2, f, half * HALF:(half + 1) * HALF], psa[n % NA][:], func,
                                                 bias=b1_s[:, v // NG, f:f + 1]).then_inc(h_kept, 1)

                pairs(act, pair)

            @block.vector
            def _(dve):
                dve.sem_inc(added, 2)

                def pair(j, last):
                    for v in range(PER):
                        for t in range(GT):
                            r = (j * PER + v) * GT + t
                            tile = (v % NG) * GT + t
                            dve.wait_ge(y_done, r + (1 + Y0))
                            dve.wait_ge(added, r + 2)
                            nc.vector.scalar_tensor_tensor(acc[:, tile, :], psb[(v * GT + t) % 2][:], gates[:, tile, bass.ds(j * 2 + v // NG, 1)],
                                                           acc[:, tile, :], ALU.mult, ALU.add).then_inc(added, 1)

                pairs(dve, pair)


def norm_affine_add(nc, K, name, y, gamma, beta):
    with Phase(nc, name) as ph:
        stat = ph.sb("stat", [P, NT, 6])
        mean, rstd, a, b = (ph.sb(s, [P, NT]) for s in ("mean", "rstd", "a", "b"))
        gb = ph.sb("gb", [P, 2, D])
        stats_done, var_ready, std_ready, dv, gb_in, normed = (ph.sem(s) for s in ("stats_done", "var_ready", "std_ready", "dv", "gb_in", "normed"))
        with nc.Block() as block:
            @block.sync
            def _(sp):
                sp.dma_start(gb[:, 0, :], over_partitions(gamma)).then_inc(gb_in, 16)
                sp.dma_start(gb[:, 1, :], over_partitions(beta)).then_inc(gb_in, 16)

            @block.vector
            def _(dve):
                ch = Chain(dve, dv)
                norm_stats(nc, dve, ch, y, ph, stats_done, var_ready, std_ready, 1e-5, stat, mean, rstd, a, b)
                dve.wait_ge(gb_in, 32)
                with dve.Fori(0, NT // UN) as i:
                    for u in range(UN):
                        t = bass.ds(i * UN + u, 1)
                        flat = y[:, t, :].rearrange("p a s -> p (a s)")
                        nc.vector.tensor_scalar(flat, flat, mean[:, t], rstd[:, t], ALU.subtract, ALU.mult).then_inc(normed, 1)
                    xs = K.x[:, bass.ds(i * UN, UN), :]
                    ys = y[:, bass.ds(i * UN, UN), :]
                    dve.wait_ge(normed, i * (UN + 2) + UN)
                    nc.vector.tensor_tensor(ys, ys, gb[:, 0, :].unsqueeze(1).to_broadcast([P, UN, D]), ALU.mult)
                    nc.vector.tensor_tensor(xs, xs, gb[:, 1, :].unsqueeze(1).to_broadcast([P, UN, D]), ALU.add).then_inc(normed, 2)
                    dve.wait_ge(normed, i * (UN + 2) + UN + 2)
                    nc.vector.tensor_tensor(xs, xs, ys, ALU.add)

            @block.scalar
            def _(act):
                act.wait_ge(var_ready, 1)
                nc.scalar.activation(b[:], a[:], ACT.Sqrt).then_inc(std_ready, 1)


def add_to_x(nc, K, name, y):
    with Phase(nc, name) as ph:
        with nc.Block() as block:
            @block.vector
            def _(dve):
                nc.vector.tensor_tensor(K.x[:], K.x[:], y[:], ALU.add)


def edge_layer(nc, K, name, w, b, edge_attr):
    SCALE = 1.0 / math.sqrt(C)
    kv_rows = nc.dram_tensor(f"{name}_kv_rows", (NPAD, 2 * D), F32, kind="Internal").ap()
    val_rows = nc.dram_tensor(f"{name}_val_rows", (STEPS, P, D), F32, kind="Internal").ap()
    with Phase(nc, name + "_attn") as keep:
        L = keep.sb("L", [P, STEPS, HEADS])
        with Phase(nc, name + "_q") as qk:
            q = qk.sb("q", [P, NT + 1, D])
            with Phase(nc, name + "_nodes") as nodes:
                xnT = nodes.sb("xnT", [P, DC, NPAD])
                with Phase(nc, name + "_xn") as xnp:
                    xn = xnp.sb("xn", [P, NT, D])
                    norm_and_transpose(nc, K, name + "_norm", K.x, xn, xnT)
                node_projections(nc, K, name + "_proj", xnT, w, b, q, kv_rows)
            edge_values(nc, K, name + "_edge", w["e"], edge_attr, kv_rows, val_rows, q, L, SCALE)
        segment_softmax(nc, K, name + "_soft", L)
        accs = [keep.sb(f"acc{n}", [P, NT + 1, ROW])[:] for n in range(2)]
        aggregate(nc, K, name + "_agg", L, accs, None, val_rows)
        finish_gat(nc, K, name + "_fin", accs, 1e-16, None, K.x)


def node_projections(nc, K, name, xnT, w, b, q, kv_rows):
    order = ["q", "k", "v", "s"]
    with Phase(nc, name) as ph:
        ws = ph.sb("w", [P, len(order), DC, D])
        bs = ph.sb("b", [P, len(order), D])
        kv = ph.sb("kv", [P, 2, 2 * D])
        ps = [ph.psum(f"ps{m}", [P, 2, D]) for m in range(4)]
        w_in, made, kept, added = (ph.sem(s) for s in ("w_in", "made", "kept", "added"))
        stored = [ph.sem(f"stored{m}") for m in range(2)]
        with nc.Block() as block:
            @block.sync
            def _(sp):
                for n, o in enumerate(order):
                    sp.dma_start(ws[:, n], w[o].rearrange("(c p) f -> p c f", p=P)).then_inc(w_in, 16)
                    sp.dma_start(bs[:, n], over_partitions(b[o])).then_inc(w_in, 16)
                for t in range(NT):
                    sp.wait_ge(kept, 2 * t + 2)
                    sp.dma_start(kv_rows[t * P:(t + 1) * P, :], kv[:, t % 2, :]).then_inc(stored[t % 2], 16)
                for m in range(2):
                    sp.wait_ge(stored[m], 16 * ((NT + 1 - m) // 2))

            @block.tensor
            def _(pe):
                pe.wait_ge(w_in, 32 * len(order))
                for t in range(NT):
                    if t >= 2:
                        pe.wait_ge(kept, 2 * t - 2)
                    for m, pair in enumerate(((0, 3), (1, 2))):
                        for a, n in enumerate(pair):
                            for c in range(DC):
                                last = nc.tensor.matmul(ps[2 * (t % 2) + m][:, a, :], xnT[:, c, t * P:(t + 1) * P], ws[:, n, c, :], start=(c == 0), stop=(c == DC - 1))
                        last.then_inc(made, 1)

            @block.vector
            def _(dve):
                nc.vector.memset(q[:, NT, :], 0.0)
                dve.wait_ge(w_in, 32 * len(order))
                for t in range(NT):
                    dve.wait_ge(made, 2 * t + 1)
                    nc.vector.tensor_tensor(q[:, t, :], ps[2 * (t % 2)][:, 0, :], bs[:, 0, :], ALU.add).then_inc(added, 1)
                    nc.vector.tensor_tensor(K.x[:, t, :], K.x[:, t, :], ps[2 * (t % 2)][:, 1, :], ALU.add).then_inc(kept, 1)
                    dve.wait_ge(made, 2 * t + 2)
                    if t >= 2:
                        dve.wait_ge(stored[t % 2], 16 * (t // 2))
                    nc.vector.tensor_tensor(kv[:, t % 2, :].rearrange("p (a f) -> p a f", a=2), ps[2 * (t % 2) + 1][:], bs[:, 1:3, :], ALU.add).then_inc(kept, 1)
                dve.wait_ge(kept, 2 * NT)
                nc.vector.tensor_tensor(K.x[:, 0:NT - 1, :], K.x[:, 0:NT - 1, :], bs[:, 3, :].unsqueeze(1).to_broadcast([P, NT - 1, D]), ALU.add)
                nc.vector.tensor_tensor(K.x[0:LAST, NT - 1, :], K.x[0:LAST, NT - 1, :], bs[0:LAST, 3, :], ALU.add)


def edge_values(nc, K, name, we, edge_attr, kv_rows, val_rows, q, L, scale):
    EB = 4
    ES = 2
    UB = 2 * ES
    NBE = STEPS // EB
    with Phase(nc, name) as ph:
        w = ph.sb("w", [P, DC, D])
        kv = ph.sb("kv", [P, UB, EB, 2 * D])
        ea = ph.sb("ea", [P, UB, EB, D])
        idx_slot = ph.sb("idx_slot", [P, UB, 2, EB], U32)
        rel_b = ph.sb("rel_b", [P, UB, EB * P], BF16)
        hot = ph.sb("hot", [P, ES, EB * P])
        eaT = ph.sb("eaT", [P, ES, EB, DC, P])
        e_s = ph.sb("e_s", [P, ES, EB, D])
        vj = ph.sb("vj", [P, ES, EB, D])
        red = ph.sb("red", [P, ES, EB, HEADS])
        ps_t = [ph.psum(f"ps_t{h}", [P, 2, DC, P]) for h in range(2)]
        ps_e = [ph.psum(f"ps_e{h}", [P, 2, D]) for h in range(2)]
        ps_q = [ph.psum(f"ps_q{m}", [P, 2, D]) for m in range(2 * ES)]
        w_in, copied, hot_built, ea_turned, eaT_kept, e_made, e_kept, q_made, kj_made, v_made, prod_made, red_made = (
            ph.sem(s) for s in ("w_in", "copied", "hot_built", "ea_turned", "eaT_kept", "e_made", "e_kept", "q_made", "kj_made", "v_made", "prod_made", "red_made"))
        claimed = ph.sem("claimed")
        kv_in = [ph.sem(f"kv_in{m}") for m in range(UB)]
        ea_in = [ph.sem(f"ea_in{m}") for m in range(UB)]
        rel_in = [ph.sem(f"rel_in{m}") for m in range(UB)]
        stored = [ph.sem(f"stored{m}") for m in range(ES)]

        def batches(eng, body):
            with eng.Fori(0, NBE // UB) as j:
                for m in range(UB):
                    body(j * UB + m, m, j * (UB // ES) + m // ES)

        with nc.Block() as block:
            @block.gpsimd
            def _(pool):
                def indices(n, slot):
                    b = bass.ds(n * EB, EB)
                    for a, table in enumerate((K.src_t, K.id_t)):
                        nc.gpsimd.tensor_tensor(idx_slot[:, slot, a, :], table[:, b], K.izero[:, 0:EB], ALU.add).then_inc(copied, 1)

                def gather(n, m, i):
                    pool.wait_ge(red_made, n + 1)
                    pool.wait_ge(ea_turned, n * 2 + 2)
                    indices(n, m)
                    pool.wait_ge(copied, n * 2 + 2)
                    pool.sem_inc(claimed, 1)
                    for u in range(EB):
                        nc.gpsimd.indirect_dma_start(out=ea[:, m, u, :], out_offset=None, in_=edge_attr,
                                                     in_offset=bass.IndirectOffsetOnAxis(ap=idx_slot[:, m, 1, u:u + 1], axis=0)).then_inc(ea_in[m], 16)
                    for u in range(EB):
                        nc.gpsimd.indirect_dma_start(out=kv[:, m, u, :], out_offset=None, in_=kv_rows,
                                                     in_offset=bass.IndirectOffsetOnAxis(ap=idx_slot[:, m, 0, u:u + 1], axis=0)).then_inc(kv_in[m], 16)

                batches(pool, gather)

            @block.sync
            def _(sp):
                sp.dma_start(w[:], we.rearrange("(c p) f -> p c f", p=P)).then_inc(w_in, 16)

                def store(n, s):
                    sp.wait_ge(v_made, n + 3)
                    sp.sem_inc(claimed, 1)
                    sp.dma_start(val_rows[bass.ds(n * EB, EB)].rearrange("s p d -> p s d"), vj[:, s]).then_inc(stored[s], 16)

                def load(n, m):
                    sp.wait_ge(hot_built, n + 1)
                    sp.sem_inc(claimed, 1)
                    sp.dma_start(rel_b[:, m, :], over_partitions(K.rel_rows[bass.ds(n * EB, EB), :].rearrange("s e -> (s e)"))).then_inc(rel_in[m], 16)

                load(0, 0)
                with sp.Fori(0, NBE // UB - 1) as j:
                    for m in range(UB):
                        load(j * UB + m + 1, (m + 1) % UB)
                        store(j * UB + m, m % ES)
                for m in range(UB):
                    if m < UB - 1:
                        load(NBE - UB + m + 1, m + 1)
                    store(NBE - UB + m, m % ES)
                for s in range(ES):
                    sp.wait_ge(stored[s], 16 * (NBE // ES) + 1)

            @block.tensor
            def _(pe):
                pe.sem_inc(q_made, 2)
                pe.sem_inc(e_made, 4)
                pe.sem_inc(ea_turned, 2 * UB)
                pe.wait_ge(w_in, 16)

                def products(n, m, i):
                    s = m % ES
                    blks = [pe.value_load(K.blk_row[0:1, bass.ds(n * EB + u, 1)], min_val=0, max_val=NT) for u in range(EB)]
                    pe.wait_ge(ea_in[m], (n - m) * (16 * EB // UB) + 16 * EB)
                    for h in range(EB // 2):
                        pe.wait_ge(eaT_kept, n * 2 + h + 1)
                        for u in range(2):
                            for c in range(DC):
                                last = nc.tensor.transpose(ps_t[h][:, u, c, :], ea[:, m, 2 * h + u, c * P:(c + 1) * P], K.ident[:])
                        last.then_inc(ea_turned, 1)
                    pe.wait_ge(hot_built, n + 1 + UB)
                    pe.wait_ge(prod_made, n + 1)
                    for u, blk in enumerate(blks):
                        last = nc.tensor.matmul(ps_q[2 * s + u // 2][:, u % 2, :], hot[:, s, u * P:(u + 1) * P],
                                                q[:, bass.ds(blk, 1), :].rearrange("p a d -> p (a d)"), start=True, stop=True)
                    last.then_inc(q_made, 1)
                    for h in range(EB // 2):
                        pe.wait_ge(eaT_kept, n * 2 + h + 3)
                        pe.wait_ge(e_kept, n * 2 + h + 1)
                        for u in range(2):
                            for c in range(DC):
                                last = nc.tensor.matmul(ps_e[h][:, u, :], eaT[:, s, 2 * h + u, c, :], w[:, c, :], start=(c == 0), stop=(c == DC - 1))
                        last.then_inc(e_made, 1)

                batches(pe, products)

            @block.scalar
            def _(act):
                act.sem_inc(eaT_kept, 2)
                act.sem_inc(e_kept, 2)

                def keep(n, m, i):
                    s = m % ES
                    for h in range(EB // 2):
                        act.wait_ge(ea_turned, n * 2 + h + 1 + 2 * UB)
                        act.wait_ge(e_made, n * 2 + 2)
                        nc.scalar.copy(eaT[:, s, 2 * h:2 * h + 2], ps_t[h][:]).then_inc(eaT_kept, 1)
                    for h in range(EB // 2):
                        act.wait_ge(e_made, n * 2 + h + 5)
                        act.wait_ge(v_made, n + 1)
                        nc.scalar.copy(e_s[:, s, 2 * h:2 * h + 2, :], ps_e[h][:]).then_inc(e_kept, 1)

                batches(act, keep)

            @block.vector
            def _(dve):
                dve.sem_inc(hot_built, UB)
                dve.sem_inc(v_made, 2)
                dve.sem_inc(prod_made, 2)
                dve.sem_inc(red_made, UB)
                for s in range(ES):
                    dve.sem_inc(stored[s], 1)

                def build(n, m):
                    dve.wait_ge(rel_in[m], (n - m) * (16 // UB) + 16)
                    dve.wait_ge(q_made, n + 1)
                    nc.vector.tensor_scalar(hot[:, m % ES, :], rel_b[:, m, :], K.row[:], None, ALU.is_equal).then_inc(hot_built, 1)

                def logits(n, m, i):
                    s = m % ES
                    dve.wait_ge(kv_in[m], (n - m) * (16 * EB // UB) + 16 * EB)
                    dve.wait_ge(e_kept, n * 2 + 4)
                    nc.vector.tensor_tensor(kv[:, m, :, 0:D], kv[:, m, :, 0:D], e_s[:, s], ALU.add).then_inc(kj_made, 1)
                    dve.wait_ge(stored[s], i * 16 + 1)
                    nc.vector.tensor_tensor(vj[:, s], kv[:, m, :, D:2 * D], e_s[:, s], ALU.add).then_inc(v_made, 1)
                    dve.wait_ge(q_made, n + 3)
                    dve.wait_ge(kj_made, n + 1)
                    for h in range(EB // 2):
                        part = kv[:, m, 2 * h:2 * h + 2, 0:D]
                        ins = nc.vector.tensor_tensor(part, part, ps_q[2 * s + h][:], ALU.mult)
                    ins.then_inc(prod_made, 1)
                    dve.wait_ge(prod_made, n + 3)
                    nc.vector.tensor_reduce(red[:, s], kv[:, m, :, 0:D].rearrange("p u (h c) -> p u h c", h=HEADS), AX.X, ALU.add).then_inc(red_made, 1)
                    dve.wait_ge(red_made, n + 1 + UB)
                    nc.vector.scalar_tensor_tensor(L[:, bass.ds(n * EB, EB), :], red[:, s], scale, bcast(K.bad_t[:, bass.ds(n * EB, EB)], HEADS),
                                                   ALU.mult, ALU.add)

                build(0, 0)
                with dve.Fori(0, NBE // UB - 1) as j:
                    for m in range(UB):
                        build(j * UB + m + 1, (m + 1) % UB)
                        logits(j * UB + m, m, j * (UB // ES) + m // ES)
                for m in range(UB):
                    n = NBE - UB + m
                    if m < UB - 1:
                        build(n + 1, m + 1)
                    logits(n, m, n // ES)


def three_layer_experts(nc, K, name, xnT, acc, gates, E, w, vec):
    NA = 4
    TA = 2 * DC
    PER = 2 * NG
    PAIRS = E // 2
    names = ("b1", "g1", "be1", "m1", "v1", "b2", "g2", "be2", "m2", "v2")
    with Phase(nc, name) as ph:
        w_s = [ph.sb(f"w{n}", [P, 2, DC, D]) for n in range(3)]
        v_s = ph.sb("vec", [P, len(names), E, DC])
        scale = ph.sb("scale", [P, 2, E, DC])
        shift = ph.sb("shift", [P, 2, E, DC])
        sc_pair = ph.sb("sc_pair", [P, 2, 2, 2, DC])
        t0 = ph.sb("t0", [P, 2, E, DC])
        t1 = ph.sb("t1", [P, 2, E, DC])
        hT = [ph.sb(f"hT{n}", [P, 2, DC, GN]) for n in range(2)]
        psa = [ph.psum(f"psa{m}", [P, HALF]) for m in range(NA)]
        psb = [ph.psum(f"psb{m}", [P, D]) for m in range(2)]
        w_in = [ph.sem(f"w_in{m}") for m in range(2)]
        v_in, dv, var_ready, std_ready, vec_ready, claimed, h_made, h_kept, y_done, added, pair_set = (
            ph.sem(n) for n in ("v_in", "dv", "var_ready", "std_ready", "vec_ready", "claimed", "h_made", "h_kept", "y_done", "added", "pair_set"))

        def pairs(eng, body):
            with eng.Fori(0, PAIRS) as j:
                body(j)

        with nc.Block() as block:
            @block.sync
            def _(sp):
                for n, v in enumerate(names):
                    sp.dma_start(v_s[:, n], vec[v].rearrange("e (c p) -> p e c", p=P)).then_inc(v_in, 16)

                def load(j):
                    for a in range(2):
                        e = j * 2 + a
                        sp.wait_ge(y_done, e * (NG * GT) + (Y0 - NG * GT))
                        sp.sem_inc(claimed, 1)
                        for n in range(3):
                            sp.dma_start(w_s[n][:, a], w[n][bass.ds(e, 1)].rearrange("a (c p) f -> p (a c) f", p=P)).then_inc(w_in[a], 16)

                pairs(sp, load)

            @block.vector
            def _(dve):
                ch = Chain(dve, dv)
                dve.sem_inc(added, 2)
                dve.wait_ge(v_in, 16 * len(names))
                for l in range(2):
                    ch.note(nc.vector.tensor_scalar(t0[:, l], v_s[:, 5 * l + 4], 0.001, None, ALU.add))
                ch.settle()
                dve.sem_inc(var_ready, 1)
                dve.wait_ge(std_ready, 1)
                ch.link(nc.vector.reciprocal(t1[:], t1[:]))
                ch.link(nc.vector.tensor_tensor(scale[:], t1[:], t1[:], ALU.mult))
                ch.link(nc.vector.tensor_tensor(scale[:], scale[:], t0[:], ALU.mult))
                ch.link(nc.vector.tensor_scalar(scale[:], scale[:], -0.5, 1.5, ALU.mult, ALU.add))
                ch.link(nc.vector.tensor_tensor(t1[:], scale[:], t1[:], ALU.mult))
                for l in range(2):
                    ch.note(nc.vector.tensor_tensor(scale[:, l], t1[:, l], v_s[:, 5 * l + 1], ALU.mult))
                    ch.note(nc.vector.tensor_tensor(t0[:, l], v_s[:, 5 * l], v_s[:, 5 * l + 3], ALU.subtract))
                ch.settle()
                ch.link(nc.vector.tensor_tensor(shift[:], t0[:], scale[:], ALU.mult))
                for l in range(2):
                    ch.note(nc.vector.tensor_tensor(shift[:, l], shift[:, l], v_s[:, 5 * l + 2], ALU.add))
                ch.settle()

                def pair(j):
                    dve.wait_ge(h_kept, j * (PER * 2 * TA) + NA)
                    for a, frm in enumerate((scale, shift)):
                        for l in range(2):
                            nc.vector.tensor_copy(sc_pair[:, a, l], frm[:, l, bass.ds(j * 2, 2), :]).then_inc(pair_set, 1)
                    for v in range(PER):
                        for t in range(GT):
                            r = (j * PER + v) * GT + t
                            tile = (v % NG) * GT + t
                            dve.wait_ge(y_done, r + (1 + Y0))
                            dve.wait_ge(added, r + 2)
                            nc.vector.scalar_tensor_tensor(acc[:, tile, :], psb[(v * GT + t) % 2][:], gates[:, tile, bass.ds(j * 2 + v // NG, 1)],
                                                           acc[:, tile, :], ALU.mult, ALU.add).then_inc(added, 1)

                pairs(dve, pair)

            @block.tensor
            def _(pe):
                pe.sem_inc(y_done, Y0)

                def hidden(l, u, v, j):
                    a, g = v // NG, v % NG
                    if l == 0 and g == 0:
                        pe.wait_ge(w_in[a], j * 48 + 48)
                    for n in range(TA):
                        f, half = n // 2, n % 2
                        q = u * (2 * TA) + l * TA + n
                        pe.wait_ge(h_kept, q + 1)
                        if l == 1:
                            pe.wait_ge(h_kept, u * (2 * TA) + TA + NA)
                        at = half * HALF
                        for c in range(DC):
                            rhs = xnT[:, c, g * GN + at:g * GN + at + HALF] if l == 0 else hT[0][:, v % 2, c, at:at + HALF]
                            last = nc.tensor.matmul(psa[n % NA][:], w_s[l][:, a, c, f * P:(f + 1) * P], rhs, start=(c == 0), stop=(c == DC - 1))
                        last.then_inc(h_made, 1)

                def output(u, v):
                    a = v // NG
                    pe.wait_ge(h_kept, u * (2 * TA) + 2 * TA + NA)
                    for t in range(GT):
                        pe.wait_ge(added, u * GT + t + 1)
                        for c in range(DC):
                            last = nc.tensor.matmul(psb[(v * GT + t) % 2][:], hT[1][:, v % 2, c, t * P:(t + 1) * P], w_s[2][:, a, c, :],
                                                    start=(c == 0), stop=(c == DC - 1))
                        last.then_inc(y_done, 1)

                def pair(j):
                    for v in range(PER):
                        u = j * PER + v
                        hidden(0, u, v, j)
                        if v:
                            output(u - 1, v - 1)
                        hidden(1, u, v, j)
                    output(j * PER + PER - 1, PER - 1)

                pairs(pe, pair)

            @block.scalar
            def _(act):
                act.sem_inc(h_kept, NA)
                act.wait_ge(var_ready, 1)
                nc.scalar.activation(t1[:], t0[:], ACT.Sqrt).then_inc(std_ready, 1)

                def pair(j):
                    act.wait_ge(pair_set, j * 4 + 4)
                    for v in range(PER):
                        u = j * PER + v
                        act.wait_ge(y_done, u * GT + (Y0 - GT))
                        for l in range(2):
                            for n in range(TA):
                                f, half = n // 2, n % 2
                                act.wait_ge(h_made, u * (2 * TA) + l * TA + n + 1)
                                nc.scalar.activation(hT[l][:, v % 2, f, half * HALF:(half + 1) * HALF], psa[n % NA][:], ACT.Relu,
                                                     bias=sc_pair[:, 1, l, v // NG, f:f + 1], scale=sc_pair[:, 0, l, v // NG, f:f + 1]).then_inc(h_kept, 1)

                pairs(act, pair)


G_EDGES = 65536
GH, GE = 4, 4
GV = GH * GE + GH
GTILES = G_EDGES // P
GB = 8
SHIFT_ROOM = 50.0


def gate_graph(nc, K, name, xnT, w_gat, att, b_gat, gamma, beta, edge_index, gates):
    src_rows = nc.dram_tensor(f"{name}_src_rows", (NPAD, GV), F32, kind="Internal").ap()
    dst_rows = nc.dram_tensor(f"{name}_dst_rows", (NPAD, 2 * GH), F32, kind="Internal").ap()
    with Phase(nc, name) as keep:
        nb = keep.sb("nb", [P, NT, GV + 2 * GH])
        agg = keep.sb("agg", [P, NT, GV])
        gate_nodes(nc, K, name + "_nodes", xnT, w_gat, att, nb, src_rows, dst_rows)
        gate_edges(nc, K, name + "_edges", edge_index, nb, src_rows, dst_rows, agg)
        gate_scores(nc, K, name + "_scores", agg, b_gat, gamma, beta, gates)


def gate_nodes(nc, K, name, xnT, w_gat, att, nb, src_rows, dst_rows):
    W = GH * GE
    with Phase(nc, name) as ph:
        w = ph.sb("w", [P, DC, GV + GH])
        a_b = ph.sb("a_b", [P, 2, W])
        prod = ph.sb("prod", [P, 2, DC, W])
        top = ph.sb("top", [P, GH])
        top_h = ph.sb("top_h", [GH, 1])
        diag = ph.sb("diag", [GH, GH])
        top_all = ph.sb("top_all", [P, GH])
        z = ph.sb("z", [P, NT, GH])
        HB = 13
        ps = [ph.psum(f"ps{m}", [P, HB, GV + GH]) for m in range(2)]
        ps_t = ph.psum("ps_t", [GH, P])
        ps_b = ph.psum("ps_b", [P, GH])
        w_in, w_ready, dv, made, top_ready, turned, diag_ready, spread, nb_ready, stored = (
            ph.sem(s) for s in ("w_in", "w_ready", "dv", "made", "top_ready", "turned", "diag_ready", "spread", "nb_ready", "stored"))
        with nc.Block() as block:
            @block.sync
            def _(sp):
                sp.dma_start(w[:, :, 0:W], w_gat.rearrange("(c p) f -> p c f", p=P)).then_inc(w_in, 16)
                for a in range(2):
                    sp.dma_start(a_b[:, a], over_partitions(att[a])).then_inc(w_in, 16)
                sp.wait_ge(nb_ready, 1)
                sp.dma_start(src_rows.rearrange("(t p) f -> p t f", p=P), nb[:, :, 0:GV]).then_inc(stored, 16)
                sp.dma_start(dst_rows.rearrange("(t p) f -> p t f", p=P), nb[:, :, GV:GV + 2 * GH]).then_inc(stored, 16)
                sp.wait_ge(stored, 32)

            @block.vector
            def _(dve):
                ch = Chain(dve, dv)
                dve.wait_ge(w_in, 48)
                for a in range(2):
                    for c in range(DC):
                        ch.note(nc.vector.tensor_tensor(prod[:, a, c], w[:, c, 0:W], a_b[:, a], ALU.mult))
                ch.settle()
                for a in range(2):
                    nc.vector.tensor_reduce(w[:, :, W + a * GH:W + (a + 1) * GH], prod[:, a].rearrange("p c (h f) -> p c h f", h=GH), AX.X, ALU.add).then_inc(w_ready, 1)
                dve.wait_ge(made, 1)
                ch.note(nc.vector.tensor_copy(nb[:, 0:HB, 0:GV + GH], ps[0][:]))
                ch.note(nc.vector.tensor_copy(nb[:, HB:NT, 0:GV + GH], ps[1][:, 0:NT - HB, :]))
                ch.settle()
                nc.vector.tensor_reduce(top[:], nb[:, :, W:GV].rearrange("p t h -> p h t"), AX.X, ALU.max).then_inc(top_ready, 1)
                dve.wait_ge(turned, 1)
                ch.link(nc.vector.tensor_reduce(top_h[:], ps_t[:], AX.X, ALU.max))
                nc.vector.tensor_scalar(diag[:], K.ident[0:GH, 0:GH], top_h[:], None, ALU.mult).then_inc(diag_ready, 1)
                dve.wait_ge(spread, 1)
                ch.link(nc.vector.tensor_copy(top_all[:], ps_b[:]))
                ch.link(nc.vector.tensor_tensor(z[:], nb[:, :, GV:GV + GH], top_all[:].unsqueeze(1).to_broadcast([P, NT, GH]), ALU.add))
                ch.link(nc.vector.scalar_tensor_tensor(nb[:, :, GV + GH:GV + 2 * GH], z[:], 0.2, z[:], ALU.mult, ALU.max))
                nc.vector.tensor_scalar(nb[:, :, GV + GH:GV + 2 * GH], nb[:, :, GV + GH:GV + 2 * GH], SHIFT_ROOM, None, ALU.subtract).then_inc(nb_ready, 1)

            @block.tensor
            def _(pe):
                pe.wait_ge(w_ready, 2)
                for t in range(NT):
                    for c in range(DC):
                        last = nc.tensor.matmul(ps[t // HB][:, t % HB, :], xnT[:, c, t * P:(t + 1) * P], w[:, c, :], start=(c == 0), stop=(c == DC - 1))
                last.then_inc(made, 1)
                pe.wait_ge(top_ready, 1)
                nc.tensor.transpose(ps_t[:], top[:], K.ident[:]).then_inc(turned, 1)
                pe.wait_ge(diag_ready, 1)
                nc.tensor.matmul(ps_b[:], K.ones[0:GH, :], diag[:], start=True, stop=True).then_inc(spread, 1)


def gate_edges(nc, K, name, edge_index, nb, src_rows, dst_rows, agg):
    W = GH * GE
    UB = 4
    NBG = GTILES // GB
    with Phase(nc, name) as ph:
        e_i = ph.sb("e_i", [P, 2, GTILES], I32)
        hi_i = ph.sb("hi_i", [P, GTILES], I32)
        e_f = ph.sb("e_f", [P, 2, GTILES])
        idx = ph.sb("idx", [P, 2, GTILES + GB], U32)
        hi = ph.sb("hi", [P, GTILES])
        lo = ph.sb("lo", [P, GTILES])
        idx_slot = ph.sb("idx_slot", [P, UB, 2, GB], U32)
        srow = ph.sb("srow", [P, 2, GB, GV])
        drow = ph.sb("drow", [P, 2, GB, 2 * GH])
        z = ph.sb("z", [P, 2, GB, GH])
        val = ph.sb("val", [P, 2, GB, GV])
        hot_lo = ph.sb("hot_lo", [P, 2, GB, P])
        hot_hi = ph.sb("hot_hi", [P, 2, GB, NT])
        wide = ph.sb("wide", [P, 2, GB, NT, GV])
        zero = ph.sb("zero", [P, NT * GV])
        ps = ph.psum("ps", [P, NT, GV])
        e_in, dv, tables, copied, freed, z_made, p_made, wide_made, summed, loops, total, zm = (
            ph.sem(s) for s in ("e_in", "dv", "tables", "copied", "freed", "z_made", "p_made", "wide_made", "summed", "loops", "total", "zm"))
        s_in = [ph.sem(f"s_in{m}") for m in range(2)]
        d_in = [ph.sem(f"d_in{m}") for m in range(2)]

        def batches(eng, body):
            with eng.Fori(0, NBG // UB) as j:
                for m in range(UB):
                    body(j * UB + m, m, j * 2 + m // 2)

        with nc.Block() as block:
            @block.sync
            def _(sp):
                sp.dma_start(e_i[:], edge_index.rearrange("a (p t) -> p a t", p=P)).then_inc(e_in, 16)

            @block.gpsimd
            def _(pool):
                pool.wait_ge(tables, 1)

                def indices(n, slot):
                    for a in range(2):
                        nc.gpsimd.tensor_tensor(idx_slot[:, slot, a, :], idx[:, a, bass.ds(n * GB, GB)], K.izero[:, 0:GB], ALU.add).then_inc(copied, 1)

                indices(0, 0)

                def gather(n, m, i):
                    pool.wait_ge(copied, n * 2 + 2)
                    pool.wait_ge(freed, n + 1)
                    indices(n + 1, (m + 1) % UB)
                    for a, (rows, to, done) in enumerate(((src_rows, srow, s_in), (dst_rows, drow, d_in))):
                        for u in range(GB):
                            nc.gpsimd.indirect_dma_start(out=to[:, m % 2, u, :], out_offset=None, in_=rows,
                                                         in_offset=bass.IndirectOffsetOnAxis(ap=idx_slot[:, m, a, u:u + 1], axis=0)).then_inc(done[m % 2], 16)

                batches(pool, gather)

            @block.vector
            def _(dve):
                ch = Chain(dve, dv)
                dve.sem_inc(freed, 2)
                dve.wait_ge(e_in, 16)
                ch.note(nc.vector.tensor_copy(e_f[:], e_i[:]))
                ch.note(nc.vector.memset(idx[:, :, GTILES:GTILES + GB], 0))
                ch.link(nc.vector.tensor_scalar(hi_i[:], e_i[:, 1, :], 7, None, ALU.arith_shift_right))
                ch.link(nc.vector.tensor_copy(hi[:], hi_i[:]))
                ch.note(nc.vector.scalar_tensor_tensor(lo[:], hi[:], -float(P), e_f[:, 1, :], ALU.mult, ALU.add))
                nc.vector.tensor_scalar(idx[:, :, 0:GTILES], e_f[:], float(N_NODES - 1), None, ALU.min).then_inc(tables, 1)
                ch.note(nc.vector.memset(zero[:], 0.0))
                ch.link(nc.vector.tensor_tensor(wide[:, 0, 0, :, 0:GH], nb[:, :, W:GV], nb[:, :, GV:GV + GH], ALU.add))
                ch.link(nc.vector.scalar_tensor_tensor(wide[:, 0, 0, :, GH:2 * GH], wide[:, 0, 0, :, 0:GH], 0.2, wide[:, 0, 0, :, 0:GH], ALU.mult, ALU.max))
                ch.link(nc.vector.tensor_tensor(wide[:, 0, 1, :, 0:GH], wide[:, 0, 0, :, GH:2 * GH], nb[:, :, GV + GH:GV + 2 * GH], ALU.subtract))
                dve.sem_inc(loops, 1)
                dve.wait_ge(zm, 1)
                for h in range(GH):
                    ch.note(nc.vector.tensor_tensor(wide[:, 0, 0, :, h * GE:(h + 1) * GE], nb[:, :, h * GE:(h + 1) * GE],
                                                    bcast(wide[:, 0, 1, :, GH + h], GE), ALU.mult))
                ch.note(nc.vector.tensor_copy(wide[:, 0, 0, :, W:GV], wide[:, 0, 1, :, GH:2 * GH]))
                ch.settle()
                dve.sem_inc(loops, 1)

                def weigh(n, m, i):
                    s = m % 2
                    dve.wait_ge(s_in[s], i * (16 * GB) + 16 * GB)
                    dve.wait_ge(d_in[s], i * (16 * GB) + 16 * GB)
                    nc.vector.tensor_tensor(z[:, s], srow[:, s, :, W:GV], drow[:, s, :, 0:GH], ALU.add).then_inc(dv, 1)
                    dve.wait_ge(dv, n * 3 + (ch.n + 1))
                    nc.vector.scalar_tensor_tensor(val[:, s, :, 0:GH], z[:, s], 0.2, z[:, s], ALU.mult, ALU.max).then_inc(dv, 1)
                    dve.wait_ge(dv, n * 3 + (ch.n + 2))
                    nc.vector.tensor_tensor(z[:, s], val[:, s, :, 0:GH], drow[:, s, :, GH:2 * GH], ALU.subtract).then_inc(z_made, 1)
                    dve.wait_ge(summed, n * GB + GB + 1)
                    nc.vector.tensor_tensor(hot_lo[:, s], K.col[:].unsqueeze(1).to_broadcast([P, GB, P]),
                                            bcast(lo[:, bass.ds(n * GB, GB)], P), ALU.is_equal)
                    nc.vector.tensor_tensor(hot_hi[:, s], K.col[:, 0:NT].unsqueeze(1).to_broadcast([P, GB, NT]),
                                            bcast(hi[:, bass.ds(n * GB, GB)], NT), ALU.is_equal)
                    dve.wait_ge(p_made, n + 1)
                    nc.vector.tensor_tensor(val[:, s, :, 0:W].rearrange("p u (h e) -> p u h e", h=GH),
                                            srow[:, s, :, 0:W].rearrange("p u (h e) -> p u h e", h=GH), bcast(z[:, s], GE), ALU.mult).then_inc(freed, 1)
                    nc.vector.tensor_copy(val[:, s, :, W:GV], z[:, s]).then_inc(dv, 1)
                    dve.wait_ge(dv, n * 3 + (ch.n + 3))
                    for u in range(GB):
                        ins = nc.vector.tensor_tensor(wide[:, s, u], bcast(hot_hi[:, s, u, :], GV), val[:, s, u, :].unsqueeze(1).to_broadcast([P, NT, GV]), ALU.mult)
                    ins.then_inc(wide_made, 1)

                batches(dve, weigh)
                dve.wait_ge(total, 1)
                nc.vector.tensor_copy(agg[:], ps[:])

            @block.scalar
            def _(act):
                act.wait_ge(loops, 1)
                nc.scalar.activation(wide[:, 0, 1, :, GH:2 * GH], wide[:, 0, 1, :, 0:GH], ACT.Exp).then_inc(zm, 1)

                def exps(n, m, i):
                    act.wait_ge(z_made, n + 1)
                    nc.scalar.activation(z[:, m % 2], z[:, m % 2], ACT.Exp).then_inc(p_made, 1)

                batches(act, exps)

            @block.tensor
            def _(pe):
                pe.wait_ge(loops, 2)
                flat = ps[:].rearrange("p t f -> p (t f)")
                nc.tensor.matmul(flat, K.ident[:], wide[:, 0, 0].rearrange("p t f -> p (t f)"), start=True, stop=False).then_inc(summed, 1 + 2 * GB)

                def sums(n, m, i):
                    pe.wait_ge(wide_made, n + 1)
                    for u in range(GB):
                        nc.tensor.matmul(flat, hot_lo[:, m % 2, u, :], wide[:, m % 2, u].rearrange("p t f -> p (t f)"),
                                         start=False, stop=False).then_inc(summed, 1)

                batches(pe, sums)
                nc.tensor.matmul(flat, K.ident[:], zero[:], start=False, stop=True).then_inc(total, 1)


def gate_scores(nc, K, name, agg, b_gat, gamma, beta, gates):
    W = GH * GE
    with Phase(nc, name) as ph:
        vb = ph.sb("vb", [P, 3, W])
        y = ph.sb("y", [P, NT, W])
        y2 = ph.sb("y2", [P, NT, W])
        r, mean, var, std = (ph.sb(s, [P, NT]) for s in ("r", "mean", "var", "std"))
        den = ph.sb("den", [P, NT, GH])
        lg = ph.sb("lg", [P, NT, 8])
        v_in, dv, var_ready, std_ready = (ph.sem(s) for s in ("v_in", "dv", "var_ready", "std_ready"))
        with nc.Block() as block:
            @block.sync
            def _(sp):
                for n, v in enumerate((b_gat, gamma, beta)):
                    sp.dma_start(vb[:, n], over_partitions(v)).then_inc(v_in, 16)

            @block.vector
            def _(dve):
                ch = Chain(dve, dv)

                def rows(n):
                    return vb[:, n].unsqueeze(1).to_broadcast([P, NT, W])

                dve.wait_ge(v_in, 48)
                ch.link(nc.vector.tensor_scalar(den[:], agg[:, :, W:GV], 1e-16, None, ALU.add))
                ch.link(nc.vector.reciprocal(den[:], den[:]))
                for h in range(GH):
                    ch.note(nc.vector.tensor_tensor(y[:, :, h * GE:(h + 1) * GE], agg[:, :, h * GE:(h + 1) * GE], bcast(den[:, :, h], GE), ALU.mult))
                ch.settle()
                ch.link(nc.vector.tensor_tensor(y[:], y[:], rows(0), ALU.add))
                ch.link(nc.vector.tensor_reduce(r[:], y[:], AX.X, ALU.add))
                ch.link(nc.vector.tensor_scalar(mean[:], r[:], 1.0 / W, None, ALU.mult))
                ch.link(nc.vector.tensor_tensor(y[:], y[:], bcast(mean[:], W), ALU.subtract))
                ch.link(nc.vector.tensor_tensor(y2[:], y[:], y[:], ALU.mult))
                ch.link(nc.vector.tensor_reduce(r[:], y2[:], AX.X, ALU.add))
                nc.vector.tensor_scalar(var[:], r[:], 1.0 / W, 1e-5, ALU.mult, ALU.add).then_inc(var_ready, 1)
                dve.wait_ge(std_ready, 1)
                ch.link(nc.vector.reciprocal(r[:], std[:]))
                ch.link(nc.vector.tensor_tensor(std[:], r[:], r[:], ALU.mult))
                ch.link(nc.vector.tensor_tensor(std[:], std[:], var[:], ALU.mult))
                ch.link(nc.vector.tensor_scalar(std[:], std[:], -0.5, 1.5, ALU.mult, ALU.add))
                ch.link(nc.vector.tensor_tensor(r[:], r[:], std[:], ALU.mult))
                ch.link(nc.vector.tensor_tensor(y[:], y[:], bcast(r[:], W), ALU.mult))
                ch.link(nc.vector.tensor_tensor(y[:], y[:], rows(1), ALU.mult))
                ch.link(nc.vector.tensor_tensor(y[:], y[:], rows(2), ALU.add))
                ch.note(nc.vector.memset(lg[:, :, GE:8], NEG))
                ch.link(nc.vector.tensor_reduce(lg[:, :, 0:GE], y[:].rearrange("p t (h e) -> p t e h", h=GH), AX.X, ALU.add))
                nc.vector.tensor_scalar(lg[:, :, 0:GE], lg[:, :, 0:GE], 1.0 / GH, None, ALU.mult)

            @block.scalar
            def _(act):
                act.wait_ge(var_ready, 1)
                nc.scalar.activation(std[:], var[:], ACT.Sqrt).then_inc(std_ready, 1)

        top2_gates(nc, K, name + "_top2", lg, 8, gates)


def gnn_moe_program(nc, I, out):
    with ExitStack() as stack:
        stack.enter_context(nc.allow_non_contiguous_dma(reason="small tables and transposed vectors"))
        K = Kept(nc, stack)
        load_constants(nc, K, I["x"])
        edge_schedule(nc, K, I["src"], I["dst"])

        def rows_view(w):
            return lambda c: [(lambda to: to[:, 0:D], w[c * P:(c + 1) * P].rearrange("p h f -> p (h f)"))]

        def heads_view(w):
            return lambda c: [(lambda to: to[:, 0:D].rearrange("p (h f) -> p h f", h=HEADS), w[:, c * P:(c + 1) * P, :].rearrange("h p f -> p h f"))]

        def flat(a):
            return a.rearrange("h f -> (h f)")

        def feed_forward(name, body):
            with Phase(nc, name) as ff:
                acc = ff.sb("acc", [P, NT, D])
                xnT = ff.sb("xnT", [P, DC, NPAD])
                norm_and_transpose(nc, K, name + "_norm", K.x, acc, xnT)
                body(ff, acc, xnT)

        clear_semaphores(nc)
        gat_layer(nc, K, "l0", rows_view(I["L0_gnn_W"]), [flat(I["L0_gnn_att_src"]), flat(I["L0_gnn_att_dst"])], HEADS, 1e-16,
                  I["L0_gnn_bias"], relu=True)

        def l0(ff, acc, xnT):
            E = 16
            g, lg = ff.sb("g", [P, NT, E]), ff.sb("lg", [P, NT, E])
            router_logits(nc, K, "l0_route", xnT, I["L0_ffn_gate_w"], I["L0_ffn_gate_b"], E, lg)
            top2_gates(nc, K, "l0_top2", lg, E, g)
            gated_bias(nc, K, "l0_b2", g, E, I["L0_ffn_b2"], acc, True)
            experts(nc, K, "l0_experts", xnT, acc, g, E, I["L0_ffn_w1"], I["L0_ffn_b1"], I["L0_ffn_w2"], ACT.Relu, 512)
            norm_affine_add(nc, K, "l0_out", acc, I["L0_ffn_gamma"], I["L0_ffn_beta"])

        clear_semaphores(nc)
        feed_forward("l0f", l0)

        clear_semaphores(nc)
        gat_layer(nc, K, "l1", heads_view(I["L1_gnn_W"]), [flat(I["L1_gnn_a_src"]), flat(I["L1_gnn_a_dst"])], HEADS, 1e-8, None)

        def l1(ff, acc, xnT):
            E = 8
            g, pw, picked = ff.sb("g", [P, NT, E]), ff.sb("pw", [P, NT, 2]), ff.sb("picked", [1, 2], I32)
            capacity = float(math.ceil(N_NODES * 1.25 / E))
            global_gates(nc, K, "l1_route", xnT, I["L1_ffn_Wr"], I["L1_ffn_br"], capacity, g, pw, picked)
            gated_bias(nc, K, "l1_b2", g, E, I["L1_ffn_b2"], acc, True)
            experts(nc, K, "l1_experts", xnT, acc, pw, 2, I["L1_ffn_W1"], I["L1_ffn_b1"], I["L1_ffn_W2"], ACT.Gelu, 512, picked)
            norm_affine_add(nc, K, "l1_out", acc, I["L1_ffn_gamma"], I["L1_ffn_beta"])

        clear_semaphores(nc)
        feed_forward("l1f", l1)

        clear_semaphores(nc)
        with Phase(nc, "l2") as l2p:
            room = l2p.sb("room", [P, NT + 1, D + 2 * HEADS])
            mid = room[:, 0:NT, 0:D]
            gat_layer(nc, K, "l2a", rows_view(I["L2_gnn_W1"]), [flat(I["L2_gnn_a_src1"]), flat(I["L2_gnn_a_dst1"])], HEADS, 1e-16,
                      I["L2_gnn_b1"], dst_x=mid, add=False, loops=True, odd=room[:])
            gat_layer(nc, K, "l2b", rows_view(I["L2_gnn_W2"]), [flat(I["L2_gnn_a_src2"]), flat(I["L2_gnn_a_dst2"])], 1, 1e-16,
                      I["L2_gnn_b2"], src_x=mid, norm=False, loops=True, odd=room[:])

        def l2(ff, acc, xnT):
            E = 8
            g = ff.sb("g", [P, NT, E])
            gate_graph(nc, K, "l2_gate", xnT, I["L2_ffn_W_gat"], [flat(I["L2_ffn_att_src"]), flat(I["L2_ffn_att_dst"])],
                       I["L2_ffn_b_gat"], I["L2_ffn_ln_gamma"], I["L2_ffn_ln_beta"], I["L2_ffn_edge_index"], g)
            gated_bias(nc, K, "l2_b2", g[:, :, 0:GE], GE, I["L2_ffn_b2"], acc, False)
            experts(nc, K, "l2_experts", xnT, acc, g, GE, I["L2_ffn_W1"], I["L2_ffn_b1"], I["L2_ffn_W2"], ACT.Gelu, 512)
            add_to_x(nc, K, "l2_out", acc)

        clear_semaphores(nc)
        feed_forward("l2f", l2)

        clear_semaphores(nc)
        edge_layer(nc, K, "l3", {n: I["L3_gnn_W" + n] for n in "qkves"}, {n: I["L3_gnn_b" + n] for n in "qkvs"}, I["edge_attr_256"])

        def l3(ff, acc, xnT):
            E = 8
            g, lg = ff.sb("g", [P, NT, E]), ff.sb("lg", [P, NT, E])
            router_logits(nc, K, "l3_route", xnT, I["L3_ffn_Wr"], I["L3_ffn_br"], E, lg)
            softmax_gates(nc, K, "l3_soft", lg, E, g)
            gated_bias(nc, K, "l3_bo", g, E, I["L3_ffn_bo"], acc, False)
            three_layer_experts(nc, K, "l3_experts", xnT, acc, g, E, [I["L3_ffn_" + n] for n in ("W1", "W2", "Wo")],
                                {n: I["L3_ffn_" + n] for n in ("b1", "g1", "be1", "m1", "v1", "b2", "g2", "be2", "m2", "v2")})
            add_to_x(nc, K, "l3_out", acc)

        clear_semaphores(nc)
        feed_forward("l3f", l3)

        with Phase(nc, "store") as ph:
            out_stored = ph.sem("out_stored")
            with nc.Block() as block:
                @block.sync
                def _(sp):
                    full = (NT - 1) * P
                    sp.dma_start(out[0:full, :].rearrange("(t p) d -> p t d", p=P), K.x[:, 0:NT - 1, :]).then_inc(out_stored, 16)
                    sp.dma_start(out[full:N_NODES, :], K.x[0:LAST, NT - 1, :]).then_inc(out_stored, 16)
                    sp.wait_ge(out_stored, 32)


def kernel(**inputs):
    import numpy as _np
    import concourse.bacc as _bacc
    from concourse import mybir as _mybir
    from concourse.bass_utils import run_bass_kernel_spmd as _run

    nc = _bacc.Bacc("TRN2", target_bir_lowering=False, num_devices=1)
    arrays, views = {}, {}
    for name, value in inputs.items():
        a = _np.ascontiguousarray(value)
        arrays[f"in_{name}"] = a
        views[name] = nc.dram_tensor(f"in_{name}", a.shape, _mybir.dt.from_np(a.dtype), kind="ExternalInput").ap()
    out = nc.dram_tensor("out_x", (N_NODES, D), _mybir.dt.float32, kind="ExternalOutput").ap()
    gnn_moe_program(nc, views, out)
    r = _run(nc, [arrays], core_ids=[0])
    return r.results[0]["out_x"]
```
